# Optimizing a Trainium2 kernel written in Bass

```python
import numpy as np
import jax
import jax.numpy as jnp

def _softmax(x, axis=-1):
    return jax.nn.softmax(x, axis=axis)

def _gelu(x):
    return jax.nn.gelu(x, approximate=True)

def _silu(x):
    return jax.nn.silu(x)

def _sigmoid(x):
    return jax.nn.sigmoid(x)

def _layernorm(x, axis=-1, eps=1e-05):
    m = jnp.mean(x, axis=axis, keepdims=True)
    v = jnp.var(x, axis=axis, keepdims=True)
    return (x - m) / jnp.sqrt(v + eps)

def _scatter_add(tgt, idx, src, axis=0):
    return tgt.at[idx].add(src)

def _segment_sum(src, seg, n):
    return jax.ops.segment_sum(src, seg, n)
kernel_name = 'mk_conv_attn_hybrid_d2_conv_nhwc768_r2_0d33f8'

def setup_inputs(seed: int=0):
    np.random.seed(seed)
    _w = jnp.asarray

    def _rec_inputs():
        import jax
        import jax.numpy as jnp
        _gk = jax.random.key(seed)
        x = -0.0005963 + 1.001 * jax.random.normal(jax.random.fold_in(_gk, 1), (1, 32, 32, 384), jnp.float32)
        return x
    x = _rec_inputs()

    def _L0_conv_setup():
        import jax, jax.numpy as jnp
        import numpy as np

        def _rel_pos_idx(q_size, k_size):
            q_coords = jnp.arange(q_size)[:, None] * max(k_size / q_size, 1.0)
            k_coords = jnp.arange(k_size)[None, :] * max(q_size / k_size, 1.0)
            rel = q_coords - k_coords + (k_size - 1) * max(q_size / k_size, 1.0)
            return rel.astype(jnp.int32)
        key = jax.random.key(seed)
        ks = jax.random.split(key, 7)
        dim, nh, H, W = (384, 12, 32, 32)
        hd = dim // nh
        return {'x': jax.random.normal(ks[0], (1, H, W, dim), jnp.float32), 'qkv_w': jax.random.normal(ks[1], (3 * dim, dim), jnp.float32) * 0.02, 'qkv_b': jax.random.normal(ks[2], (3 * dim,), jnp.float32) * 0.02, 'proj_w': jax.random.normal(ks[3], (dim, dim), jnp.float32) * 0.02, 'proj_b': jax.random.normal(ks[4], (dim,), jnp.float32) * 0.02, 'rel_pos_h': jax.random.normal(ks[5], (2 * H - 1, hd), jnp.float32) * 0.02, 'rel_pos_w': jax.random.normal(ks[6], (2 * W - 1, hd), jnp.float32) * 0.02, 'num_heads': nh}
    _L0_conv_all = _L0_conv_setup()
    _L0_conv_in = {k: v for k, v in _L0_conv_all.items() if k in ('qkv_w', 'qkv_b', 'proj_w', 'proj_b', 'rel_pos_h', 'rel_pos_w')}
    del _L0_conv_all

    def _L1_attn_setup():
        import jax, jax.numpy as jnp
        import numpy as np
        EMBED_DIM = 384
        NUM_HEADS = 12
        HEAD_DIM = EMBED_DIM // NUM_HEADS
        B, N = (16, 512)
        key = jax.random.key(seed)
        k1, k2, k3 = jax.random.split(key, 3)
        x = jax.random.normal(k1, (B, N, EMBED_DIM), dtype=jnp.float32)
        w_qkv = jax.random.normal(k2, (3 * EMBED_DIM, EMBED_DIM), dtype=jnp.float32) * EMBED_DIM ** (-0.5)
        w_proj = jax.random.normal(k3, (EMBED_DIM, EMBED_DIM), dtype=jnp.float32) * EMBED_DIM ** (-0.5)
        b_proj = jnp.zeros((EMBED_DIM,), dtype=jnp.float32)
        return {'x': x, 'w_qkv': w_qkv, 'w_proj': w_proj, 'b_proj': b_proj}
    _L1_attn_all = _L1_attn_setup()
    _L1_attn_in = {k: v for k, v in _L1_attn_all.items() if k in ('w_qkv', 'w_proj', 'b_proj')}
    del _L1_attn_all

    def _L1_ffn_setup():
        import jax, jax.numpy as jnp
        import numpy as np
        N_EXPERTS = 8
        TOP_K = 2
        key = jax.random.key(seed)
        ks = jax.random.split(key, 4)
        B, T, C = (8, 256, 384)
        H = 4 * C
        E = N_EXPERTS
        scale = 0.02
        x = jax.random.normal(ks[0], (B, T, C), dtype=jnp.float32)
        gate_w = jax.random.normal(ks[1], (E, C), dtype=jnp.float32) * scale
        gate_b = jnp.zeros((E,), dtype=jnp.float32)
        w1 = jax.random.normal(ks[2], (E, H, C), dtype=jnp.float32) * scale
        b1 = jnp.zeros((E, H), dtype=jnp.float32)
        w2 = jax.random.normal(ks[3], (E, C, H), dtype=jnp.float32) * scale
        b2 = jnp.zeros((E, C), dtype=jnp.float32)
        return {'x': x, 'gate_w': gate_w, 'gate_b': gate_b, 'w1': w1, 'b1': b1, 'w2': w2, 'b2': b2}
    _L1_ffn_all = _L1_ffn_setup()
    _L1_ffn_in = {k: v for k, v in _L1_ffn_all.items() if k in ('gate_w', 'gate_b', 'w1', 'b1', 'w2', 'b2')}
    del _L1_ffn_all
    return {'x': x, 'L0_conv_qkv_w': _L0_conv_in['qkv_w'], 'L0_conv_qkv_b': _L0_conv_in['qkv_b'], 'L0_conv_proj_w': _L0_conv_in['proj_w'], 'L0_conv_proj_b': _L0_conv_in['proj_b'], 'L0_conv_rel_pos_h': _L0_conv_in['rel_pos_h'], 'L0_conv_rel_pos_w': _L0_conv_in['rel_pos_w'], 'L1_attn_w_qkv': _L1_attn_in['w_qkv'], 'L1_attn_w_proj': _L1_attn_in['w_proj'], 'L1_attn_b_proj': _L1_attn_in['b_proj'], 'L1_ffn_gate_w': _L1_ffn_in['gate_w'], 'L1_ffn_gate_b': _L1_ffn_in['gate_b'], 'L1_ffn_w1': _L1_ffn_in['w1'], 'L1_ffn_b1': _L1_ffn_in['b1'], 'L1_ffn_w2': _L1_ffn_in['w2'], 'L1_ffn_b2': _L1_ffn_in['b2']}

def reference(x, L0_conv_qkv_w, L0_conv_qkv_b, L0_conv_proj_w, L0_conv_proj_b, L0_conv_rel_pos_h, L0_conv_rel_pos_w, L1_attn_w_qkv, L1_attn_w_proj, L1_attn_b_proj, L1_ffn_gate_w, L1_ffn_gate_b, L1_ffn_w1, L1_ffn_b1, L1_ffn_w2, L1_ffn_b2):
    import jax
    import jax.numpy as jnp

    def _L0_conv_ref(x, qkv_w, qkv_b, proj_w, proj_b, rel_pos_h, rel_pos_w, num_heads):
        import jax, jax.numpy as jnp
        import numpy as np

        def _rel_pos_idx(q_size, k_size):
            q_coords = jnp.arange(q_size)[:, None] * max(k_size / q_size, 1.0)
            k_coords = jnp.arange(k_size)[None, :] * max(q_size / k_size, 1.0)
            rel = q_coords - k_coords + (k_size - 1) * max(q_size / k_size, 1.0)
            return rel.astype(jnp.int32)
        b, h, w, c = x.shape
        nh = num_heads
        hd = c // nh
        scale = hd ** (-0.5)
        hw = h * w
        qkv = (x.reshape(b, hw, c) @ qkv_w.T + qkv_b).reshape(b, hw, 3, nh, hd)
        qkv = jnp.transpose(qkv, (2, 0, 3, 1, 4)).reshape(3, b * nh, hw, hd)
        q, k, v = (qkv[0], qkv[1], qkv[2])
        attn = jnp.einsum('bqd,bkd->bqk', q * scale, k)
        rh = rel_pos_h[_rel_pos_idx(h, h)]
        rw = rel_pos_w[_rel_pos_idx(w, w)]
        r_q = q.reshape(b * nh, h, w, hd)
        rel_h = jnp.einsum('bhwc,hkc->bhwk', r_q, rh)
        rel_w = jnp.einsum('bhwc,wkc->bhwk', r_q, rw)
        attn = attn.reshape(b * nh, h, w, h, w) + rel_h[:, :, :, :, None] + rel_w[:, :, :, None, :]
        attn = attn.reshape(b * nh, hw, hw)
        attn = jax.nn.softmax(attn, axis=-1)
        out = jnp.einsum('bqk,bkd->bqd', attn, v)
        out = out.reshape(b, nh, h, w, hd)
        out = jnp.transpose(out, (0, 2, 3, 1, 4)).reshape(b, h, w, c)
        return out @ proj_w.T + proj_b

    def _L1_attn_ref(x, w_qkv, w_proj, b_proj):
        import jax, jax.numpy as jnp
        import numpy as np
        EMBED_DIM = 384
        NUM_HEADS = 12
        HEAD_DIM = EMBED_DIM // NUM_HEADS
        B, N = (16, 512)
        b, n, d = x.shape
        h, dh = (NUM_HEADS, HEAD_DIM)
        qkv = jnp.einsum('bnd,ed->bne', x, w_qkv)
        qkv = qkv.reshape(b, n, 3, h, dh).transpose(2, 0, 3, 1, 4)
        q, k, v = (qkv[0], qkv[1], qkv[2])
        scores = jnp.einsum('bhqd,bhkd->bhqk', q, k) / d ** 0.5
        attn = jax.nn.softmax(scores, axis=-1)
        out = jnp.einsum('bhqk,bhkd->bhqd', attn, v)
        out = out.transpose(0, 2, 1, 3).reshape(b, n, d)
        return jnp.einsum('bnd,ed->bne', out, w_proj) + b_proj

    def _L1_ffn_ref(x, gate_w, gate_b, w1, b1, w2, b2):
        import jax, jax.numpy as jnp
        import numpy as np
        N_EXPERTS = 8
        TOP_K = 2
        B, T, C = x.shape
        E = gate_w.shape[0]
        xr = x.reshape(B * T, C)
        N = xr.shape[0]
        logits = xr @ gate_w.T + gate_b
        probs = jax.nn.softmax(logits, axis=-1)
        topv, topi = jax.lax.top_k(probs, TOP_K)
        topv = topv / jnp.sum(topv, axis=-1, keepdims=True)
        tok_w = jnp.zeros((N, E), dtype=xr.dtype).at[jnp.arange(N)[:, None], topi].add(topv)
        out = jnp.zeros((N, C), dtype=xr.dtype)
        for e in range(E):
            h = jax.nn.relu(xr @ w1[e].T + b1[e])
            y = h @ w2[e].T + b2[e]
            out = out + tok_w[:, e:e + 1] * y
        return out.reshape(B, T, C)

    def _gn(v, G=32, eps=1e-05):
        B_, H_, W_, C_ = v.shape
        g = v.reshape(B_, H_, W_, G, C_ // G)
        m = jnp.mean(g, axis=(1, 2, 4), keepdims=True)
        s = jnp.var(g, axis=(1, 2, 4), keepdims=True)
        return ((g - m) / jnp.sqrt(s + eps)).reshape(v.shape)

    def _ln_c(v, eps=1e-06):
        m = jnp.mean(v, axis=-1, keepdims=True)
        s = jnp.var(v, axis=-1, keepdims=True)
        return (v - m) / jnp.sqrt(s + eps)

    def _ln_t(v, eps=1e-05):
        m = jnp.mean(v, axis=-1, keepdims=True)
        s = jnp.var(v, axis=-1, keepdims=True)
        return (v - m) / jnp.sqrt(s + eps)

    def _to_tokens(v):
        B_, H_, W_, C_ = v.shape
        return v.reshape(B_, H_ * W_, C_)

    def _from_tokens(t, like):
        return t.reshape(like.shape)
    x = x + _L0_conv_ref(_gn(x), L0_conv_qkv_w, L0_conv_qkv_b, L0_conv_proj_w, L0_conv_proj_b, L0_conv_rel_pos_h, L0_conv_rel_pos_w, 12)
    t = _to_tokens(x)
    t = t + _L1_attn_ref(_ln_t(t), L1_attn_w_qkv, L1_attn_w_proj, L1_attn_b_proj)
    t = t + _L1_ffn_ref(_ln_t(t), L1_ffn_gate_w, L1_ffn_gate_b, L1_ffn_w1, L1_ffn_b1, L1_ffn_w2, L1_ffn_b2)
    x = _from_tokens(t, x)
    return x

_drawn_inputs = setup_inputs


def setup_inputs(seed=0):
    import zlib

    import numpy as np

    out = dict(_drawn_inputs(seed))
    spreads = {'L1_attn_b_proj': (0.0, 0.1),
     'L1_ffn_gate_b': (0.0, 0.1),
     'L1_ffn_b1': (0.0, 0.1),
     'L1_ffn_b2': (0.0, 0.1)}
    factors = {'L0_conv_qkv_b': 2.868, 'L0_conv_rel_pos_h': 54.112, 'L0_conv_rel_pos_w': 47.287}
    for name, (base, spread) in spreads.items():
        noise = np.random.default_rng([zlib.crc32(name.encode()), seed]).standard_normal(out[name].shape)
        drawn = base * np.exp(spread * noise) if base else spread * noise
        out[name] = jnp.asarray(drawn.astype(out[name].dtype))
    for name, factor in factors.items():
        out[name] = (out[name] * factor).astype(out[name].dtype)
    return out
```

```python
from contextlib import ExitStack

import numpy as np
import concourse.bass as bass
from concourse import mybir

F32 = mybir.dt.float32
F32R = mybir.dt.float32r
ALU = mybir.AluOpType
ACT = mybir.ActivationFunctionType
AX = mybir.AxisListType

P = 128
C = 384
KT = C // P
SIDE = 32
N = SIDE * SIDE
TT = N // P
NH = 12
HD = C // NH
HALF = 512
NE = 8
HID = 4 * C
HC = HID // P
GROUP = C // 32
REL = 2 * SIDE - 1
SCALE = (HD ** -0.5, C ** -0.5)
NP = 4

Q_LO, Q_HI, RH_HI, RW_HI, RH_LO, RW_LO, K_HI, K_LO = range(8)


def build_program(nc, a):
    ctx = ExitStack()
    with ctx:
        def sem(name):
            return ctx.enter_context(nc.semaphore(name))

        def sb(name, shape, dt=F32, where=ctx):
            return where.enter_context(nc.sbuf_tensor(name, shape, dt))

        ps = ctx.enter_context(nc.psum_tensor("ps", [P, 8, HALF], F32))

        heads_dram = [nc.dram_tensor(f"heads{L}", [8, C, N], F32).ap() for L in range(2)]
        v_dram = [nc.dram_tensor(f"v{L}", [NH, P, TT, HD], F32).ap() for L in range(2)]
        att_dram = [nc.dram_tensor(f"att{L}", [C, N], F32).ap() for L in range(2)]

        t = sb("t", [P, TT, C])
        xnT = sb("xnT", [P, KT, N])
        tn = sb("tn", [P, 2, C])
        ident = sb("ident", [P, P])
        wqkv = sb("wqkv", [P, KT, 3 * C])
        wproj = sb("wproj", [P, KT, C])
        bqk = sb("bqk", [P, 6])
        bv = sb("bv", [P, C])
        bproj = sb("bproj", [P, 2, C])
        gate = sb("gate", [P, KT, NE])
        gateb = sb("gateb", [P, NE])
        b2 = sb("b2", [1, NE, C])
        b1 = sb("b1", [P, NE, HC])
        ones = sb("ones", [P, P])
        stat = sb("stat", [P, TT, 12])
        mv = sb("mv", [P, TT, 2])
        sd = sb("sd", [P, TT])
        rstd = sb("rstd", [P, TT])
        gm = sb("gm", [P, KT, 2])
        gd = sb("gd", [P, KT])
        lg = sb("lg", [P, TT, NE])
        pr = sb("pr", [P, TT, NE])
        w8 = sb("w8", [P, TT, NE])
        rk = sb("rk", [P, TT, NE])
        cm = sb("cm", [P, TT, NE, NE])
        cm2 = sb("cm2", [P, TT, NE, NE])
        low = sb("low", [P, NE, NE])
        m8 = sb("m8", [P, TT])
        s8 = sb("s8", [P, TT])

        att = ExitStack()
        qf = sb("qf", [P, KT, N], where=att)
        vf = sb("vf", [P, TT, C], where=att)
        oT = vf[:, :, :].rearrange("p a b -> p (a b)").rearrange("p (k n) -> p k n", k=KT)
        stage = sb("stage", [P, 4, N], F32R, where=att)
        kf = sb("kf", [P, 2, N], where=att)
        grp = qf[:, 0, :].rearrange("p (a b) -> p a b", b=P)
        bd = sb("bd", [P, 2, REL, 4], where=att)
        tab = sb("tab", [P, 2, REL], where=att)
        qa = [sb(f"qa{i}", [104, N], F32R, where=att) for i in range(2)]
        ka = [sb(f"ka{i}", [104, N], F32R, where=att) for i in range(2)]
        qm = [sb(f"qm{i}", [96, N], F32R, where=att) for i in range(2)]
        km = [sb(f"km{i}", [96, N], F32R, where=att) for i in range(2)]
        qb = [sb(f"qb{i}", [P, N], F32R, where=att) for i in range(2)]
        eb = sb("eb", [P, N], F32R, where=att)
        va = [sb(f"va{i}", [P, TT, 2 * HD], where=att) for i in range(2)]
        prob = sb("prob", [P, NP, N], where=att)
        mcol = sb("mcol", [P, 2, TT], where=att)
        negd = sb("negd", [TT, TT, P], where=att)
        rec = sb("rec", [HD, HALF], where=att)
        osb = [sb(f"osb{i}", [HD, N], where=att) for i in range(2)]
        ebf = prob[:, 0, :]
        att.close()
        moe = ExitStack()
        w1 = [sb(f"w1_{i}", [P, KT, HID], where=moe) for i in range(2)]
        w2 = [sb(f"w2_{i}", [P, HC, C], where=moe) for i in range(2)]
        hT = sb("hT", [P, 4, HALF], where=moe)
        moe.close()

        ld_x = sem("ld_x")
        ld_c = sem("ld_c")
        ld_w = [sem(f"ld_w{L}") for L in range(2)]
        ld_e = sem("ld_e")
        consts = sem("consts")
        bd_ok = sem("bd_ok")
        m_free = sem("m_free")
        a_free = sem("a_free")
        dv = sem("dv")
        av = sem("av")
        g_sum = sem("g_sum")
        xn_ok = [sem(f"xn_ok{L}") for L in range(3)]
        L2 = range(2)
        qk_mm = [sem(f"qk_mm{L}") for L in L2]
        qk_ev = [sem(f"qk_ev{L}") for L in L2]
        v_mm = [sem(f"v_mm{L}") for L in L2]
        v_ev = [sem(f"v_ev{L}") for L in L2]
        split = [sem(f"split{L}") for L in L2]
        st_v = [sem(f"st_v{L}") for L in L2]
        st_s = [[sem(f"st_s{L}_{i}") for i in range(4)] for L in L2]
        rel_mm = sem("rel_mm")
        rel_hi = sem("rel_hi")
        rel_ev = sem("rel_ev")
        ld_m = [[sem(f"ld_m{L}{i}") for i in L2] for L in L2]
        ld_a = [[sem(f"ld_a{L}{i}") for i in L2] for L in L2]
        sm_ok = [sem(f"sm_ok{L}") for L in L2]
        mx_ok = [sem(f"mx_ok{L}") for L in L2]
        mT_ok = [sem(f"mT_ok{L}") for L in L2]
        r_ok = [sem(f"r_ok{L}") for L in L2]
        st_ok = [sem(f"st_ok{L}") for L in L2]
        p_ok = [sem(f"p_ok{L}") for L in L2]
        pv_ok = [sem(f"pv_ok{L}") for L in L2]
        o_rc = [sem(f"o_rc{L}") for L in L2]
        o_ok = [sem(f"o_ok{L}") for L in L2]
        st_o = [[sem(f"st_o{L}{i}") for i in L2] for L in L2]
        ld_o = [sem(f"ld_o{L}") for L in L2]
        pj_mm = [sem(f"pj_mm{L}") for L in L2]
        t_ok = [sem(f"t_ok{L}") for L in L2]
        tn_ok = [sem(f"tn_ok{L}") for L in L2]
        tr_mm = [sem(f"tr_mm{L}") for L in L2]
        lg_mm = sem("lg_mm")
        lg_ev = sem("lg_ev")
        lx = sem("lx")
        w8_ok = sem("w8_ok")
        ld_1 = [sem(f"ld_1{i}") for i in L2]
        h_mm = sem("h_mm")
        h_ev = sem("h_ev")
        y_mm = sem("y_mm")
        y_ev = sem("y_ev")
        st_y = sem("st_y")

        def wait(eng, s, value):
            if not isinstance(value, int) or value > 0:
                eng.wait_ge(s, value)

        def stored(n):
            return 16 * sum(1 if i < 4 * KT else 4 for i in range(n % 4, n, 4))

        def f(ap):
            return ap.bitcast(F32)

        def hrow(eng, h):
            return bass.ds(h * HD if isinstance(h, int) else eng.snap(h * HD), HD)

        block = ctx.enter_context(nc.Block())

        @block.sync
        def _(sp):
            sp.dma_start(xnT[:], a["xT"].rearrange("(k p) n -> p k n", p=P)).then_inc(ld_x, 16)
            sp.dma_start(grp, a["grp"].rearrange("g p c -> p g c")[:, 0:8, :]).then_inc(ld_x, 16)
            sp.dma_start(qf[:, 1, 0:P], a["grp"][8]).then_inc(ld_x, 16)
            sp.dma_start(wqkv[:], a["wqkv0"].rearrange("(k p) n -> p k n", p=P)).then_inc(ld_w[0], 16)
            for dst, name in ((ident[:], "ident"), (bqk[:], "bqk"), (low[:], "low"), (negd[:], "negd"), (ebf, "eb")):
                sp.dma_start(dst, a[name]).then_inc(ld_c, 16)
            for dst, name in ((bv[:], "bv"), (bproj[:, 0, :], "bproj0"), (bproj[:, 1, :], "bproj1"),
                              (gateb[:], "gateb")):
                sp.dma_start(dst, a[name].partition_broadcast(P)).then_inc(ld_c, 16)
            sp.dma_start(t[:], a["x"].rearrange("(t p) c -> p t c", p=P)).then_inc(ld_c, 16)
            sp.dma_start(gate[:], a["gate"].rearrange("(k p) e -> p k e", p=P)).then_inc(ld_c, 16)
            sp.dma_start(b2[:], a["b2"].unsqueeze(0)).then_inc(ld_c, 16)
            sp.dma_start(b1[:], a["b1"]).then_inc(ld_c, 16)
            for i, name in enumerate(("relh", "relw")):
                for g in range(4):
                    sp.dma_start(tab[g * HD:(g + 1) * HD, i, :], a[name]).then_inc(ld_c, 16)
            sp.wait_ge(consts, 3)
            for i in L2:
                sp.dma_start(f(km[i][32:96, :]), f(eb[0:64, :])).then_inc(ld_e, 16)

            for L in L2:
                order = []
                for m in range(KT):
                    order += [(Q_HI, m), (Q_LO, m)]
                for m in range(KT):
                    order += [(K_HI, m), (K_LO, m)]
                if L == 0:
                    for hi, lo in ((RH_HI, RH_LO), (RW_HI, RW_LO)):
                        for m in range(KT):
                            order += [(hi, m), (lo, m)]
                for n, (slot, m) in enumerate(order):
                    sp.wait_ge(split[L], n + 1)
                    dst, src = heads_dram[L][slot, m * P:(m + 1) * P, :], f(stage[:, n % 4, :])
                    if slot in (RH_HI, RW_HI, RH_LO, RW_LO):
                        for g in range(4):
                            sp.dma_start(dst[g * HD:(g + 1) * HD, :], src[g:P:4, :]).then_inc(st_s[L][n % 4], 16)
                    else:
                        sp.dma_start(dst, src).then_inc(st_s[L][n % 4], 16)
                sp.wait_ge(v_ev[L], TT)
                for h in range(NH):
                    sp.dma_start(v_dram[L][h], vf[:, :, h * HD:(h + 1) * HD]).then_inc(st_v[L], 16)
                for i in range(4):
                    sp.wait_ge(st_s[L][i], stored(len(order) + i))
                sp.wait_ge(st_v[L], 16 * NH)
                H = heads_dram[L]

                def load_m(h, b):
                    rows = hrow(sp, h)
                    wait(sp, sm_ok[L], TT * (h - 1))
                    sp.sem_inc(m_free, 1)
                    sp.dma_start(f(qm[b][0:32, :]), H[Q_HI, rows, :]).then_inc(ld_m[L][b], 16)
                    sp.dma_start(f(km[b][0:32, :]), H[K_HI, rows, :]).then_inc(ld_m[L][b], 16)
                    if L == 0:
                        sp.dma_start(f(qm[b][32:64, :]), H[RH_HI, rows, :]).then_inc(ld_m[L][b], 16)
                        sp.dma_start(f(qm[b][64:96, :]), H[RW_HI, rows, :]).then_inc(ld_m[L][b], 16)

                def load_a(h, b):
                    rows = hrow(sp, h)
                    wait(sp, pv_ok[L], TT * (h - 1))
                    sp.sem_inc(a_free, 1)
                    for i, slot in enumerate((Q_LO, Q_HI, Q_HI)):
                        sp.dma_start(f(qa[b][32 * i:32 * i + 32, :]), H[slot, rows, :]).then_inc(ld_a[L][b], 16)
                    for i, slot in enumerate((K_HI, K_HI, K_LO)):
                        sp.dma_start(f(ka[b][32 * i:32 * i + 32, :]), H[slot, rows, :]).then_inc(ld_a[L][b], 16)
                    if L == 0:
                        for i, slot in enumerate((RH_HI, RW_HI, RH_LO, RW_LO)):
                            sp.dma_start(f(qb[b][32 * i:32 * i + 32, :]), H[slot, rows, :]).then_inc(ld_a[L][b], 16)
                    sp.dma_start(va[b][:, :, 0:HD], v_dram[L][bass.ds(h, 1)].rearrange("h p t d -> p (h t) d")).then_inc(ld_a[L][b], 16)

                if L == 1:
                    sp.wait_ge(pv_ok[0], TT * NH)
                load_m(0, 0)
                load_a(0, 0)
                load_m(1, 1)
                load_a(1, 1)
                load_m(2, 0)
                load_a(2, 0)
                load_m(3, 1)
                with sp.Fori(1, NH // 2 - 1) as i:
                    load_a(2 * i + 1, 1)
                    load_m(2 * i + 2, 0)
                    load_a(2 * i + 2, 0)
                    load_m(2 * i + 3, 1)
                load_a(NH - 1, 1)
                if L == 0:
                    sp.dma_start(wproj[:], a["wproj0"].rearrange("(k p) n -> p k n", p=P)).then_inc(ld_w[0], 16)
                    sp.wait_ge(v_mm[0], TT)
                    sp.dma_start(wqkv[:], a["wqkv1"].rearrange("(k p) n -> p k n", p=P)).then_inc(ld_w[1], 16)
                else:
                    sp.wait_ge(pj_mm[0], TT)
                    sp.dma_start(wproj[:], a["wproj1"].rearrange("(k p) n -> p k n", p=P)).then_inc(ld_w[1], 16)
                for i in L2:
                    sp.wait_ge(st_o[L][i], 8 * NH)
                sp.dma_start(oT, att_dram[L].rearrange("(k p) n -> p k n", p=P)).then_inc(ld_o[L], 16)

            sp.wait_ge(pj_mm[1], TT)
            for e in range(NE):
                if e >= 2:
                    sp.wait_ge(y_mm, 2 * (e - 1))
                sp.dma_start(w1[e % 2][:], a["w1"][e].rearrange("(k p) n -> p k n", p=P)).then_inc(ld_1[e % 2], 16)
                sp.dma_start(w2[e % 2][:], a["w2"][e].rearrange("(k p) n -> p k n", p=P)).then_inc(ld_1[e % 2], 16)
            for tt in range(TT):
                sp.wait_ge(y_ev, 8 * (NE - 1) + tt + 1)
                sp.dma_start(a["out"][tt * P:(tt + 1) * P, :], t[:, tt, :]).then_inc(st_y, 16)
            sp.wait_ge(st_y, 16 * TT)

        @block.tensor
        def _(pe):
            mm = pe.matmul
            for r in range(2):
                pe.wait_ge(consts, 4 + r)
                if r == 0:
                    pe.wait_ge(ld_x, 48)
                for m in range(KT):
                    for k in range(KT):
                        g = k * KT + m
                        lhs = grp[:, g, :] if g < 8 else qf[:, 1, 0:P]
                        last = mm(ps[:, r, m:m + 1], lhs, mv[:, k, 0:1] if r == 0 else gd[:, k:k + 1],
                                  start=(k == 0), stop=(k == KT - 1))
                last.then_inc(g_sum, 1)

            for L in L2:
                pe.wait_ge(xn_ok[L], KT if L == 0 else TT)
                pe.wait_ge(ld_w[L], 16)
                for u in range(2 * KT):
                    wait(pe, qk_ev[L], u - 1)
                    for half in range(2):
                        for k in range(KT):
                            last = mm(ps[:, 2 * (u % 2) + half, :], wqkv[:, k, u * P:(u + 1) * P],
                                      xnT[:, k, half * HALF:(half + 1) * HALF], start=(k == 0), stop=(k == KT - 1))
                    last.then_inc(qk_mm[L], 1)
                for tt in range(TT):
                    wait(pe, v_ev[L], tt - 3)
                    for k in range(KT):
                        last = mm(ps[:, 4 + tt % 4, 0:C], xnT[:, k, tt * P:(tt + 1) * P],
                                  wqkv[:, k, 2 * C:3 * C], start=(k == 0), stop=(k == KT - 1))
                    last.then_inc(v_mm[L], 1)
                if L == 0:
                    pe.wait_ge(qk_ev[0], 2 * KT)
                    pe.wait_ge(bd_ok, 4)
                    for w in range(2):
                        for i in range(SIDE // 4):
                            n = 8 * w + i
                            wait(pe, rel_ev, n - 3)
                            for j in range(4):
                                s = 4 * i + j
                                q = qf[:, :, :].rearrange("p g (h w) -> p g h w", w=SIDE)
                                rhs = q[:, :, s, :] if w == 0 else q[:, :, :, s]
                                last = mm(ps[:, n % 4, 96 * j:96 * j + 96], bd[:, w, SIDE - 1 - s:REL - s, :].rearrange("p i a -> p (i a)"),
                                          rhs, start=True, stop=True)
                            last.then_inc(rel_mm, 1)
                    pe.wait_ge(rel_ev, 16)
                pe.wait_ge(v_ev[L], TT)
                pe.wait_ge(qk_ev[L], 2 * KT)
                pe.wait_ge(ld_e, 32)

                n_m, n_a = (4, 11) if L == 0 else (2, 7)
                kr = 96 if L == 0 else 32

                def max_scores(h, b, qt):
                    wait(pe, mx_ok[L], TT * h + qt)
                    if qt == 0:
                        pe.wait_ge(ld_m[L][b], (h - b) * 8 * n_m + 16 * n_m)
                    for half in range(2):
                        last = mm(ps[:, half, :], qm[b][0:kr, qt * P:(qt + 1) * P],
                                  km[b][0:kr, half * HALF:(half + 1) * HALF], start=True, stop=True)
                    last.then_inc(sm_ok[L], 1)

                def turn_max(h, b):
                    pe.wait_ge(mx_ok[L], TT * (h + 1))
                    wait(pe, o_ok[L], 2 * (h - 1))
                    pe.transpose(ps[0:TT, 6 + b, 0:P], mcol[:, b, :], ident[:]).then_inc(mT_ok[L], 1)

                def scores(h, b, s):
                    if s == 0:
                        pe.wait_ge(ld_a[L][b], (h - b) * 8 * n_a + 16 * n_a)
                        pe.wait_ge(r_ok[L], h + 1)
                    wait(pe, p_ok[L], TT * h + s - 1)
                    for half in range(2):
                        out = ps[:, 2 + 2 * (s % 2) + half, :]
                        cols = slice(half * HALF, (half + 1) * HALF)
                        last = mm(out, ka[b][:, s * P:(s + 1) * P], qa[b][:, cols], start=True, stop=(L == 1))
                        if L == 0:
                            last = mm(out, eb[:, s * P:(s + 1) * P], qb[b][:, cols], start=False, stop=True)
                    last.then_inc(st_ok[L], 1)

                def out_product(h, b, s):
                    pe.wait_ge(p_ok[L], TT * h + s + 1)
                    if s == 0:
                        wait(pe, o_ok[L], 2 * (h - 1))
                    for half in range(2):
                        last = mm(ps[64 * half:64 * half + 64, 6 + b, :], va[b][:, s, :],
                                  prob[:, s % NP, half * HALF:(half + 1) * HALF], start=(s == 0), stop=(s == TT - 1))
                    last.then_inc(pv_ok[L], 1)

                def head(h, b, first=False, left=2):
                    for s in range(TT):
                        scores(h, b, s)
                        if s < 6 and left >= 1:
                            max_scores(h + 1, 1 - b, s + 2)
                        if s == 7 and left >= 1:
                            turn_max(h + 1, 1 - b)
                        if s >= 6 and left >= 2:
                            max_scores(h + 2, b, s - 6)
                        if s > 0:
                            out_product(h, b, s - 1)
                        elif not first:
                            out_product(h - 1, 1 - b, TT - 1)

                for m in range(TT):
                    max_scores(0, 0, m)
                turn_max(0, 0)
                max_scores(1, 1, 0)
                max_scores(1, 1, 1)
                head(0, 0, first=True)
                head(1, 1)
                with pe.Fori(1, NH // 2 - 1) as i:
                    head(2 * i, 0)
                    head(2 * i + 1, 1)
                head(NH - 2, 0, left=1)
                head(NH - 1, 1, left=0)
                out_product(NH - 1, 1, TT - 1)

                pe.wait_ge(o_ok[L], 2 * NH)
                pe.wait_ge(ld_o[L], 16)
                pe.wait_ge(ld_w[L], 32)
                for tt in range(TT):
                    wait(pe, t_ok[L], tt - 3)
                    for k in range(KT):
                        last = mm(ps[:, tt % 4, 0:C], oT[:, k, tt * P:(tt + 1) * P], wproj[:, k, :],
                                  start=(k == 0), stop=(k == KT - 1))
                    last.then_inc(pj_mm[L], 1)
                for tt in range(TT):
                    pe.wait_ge(tn_ok[L], tt + 1)
                    wait(pe, xn_ok[L + 1], tt - 1)
                    for k in range(KT):
                        last = pe.transpose(ps[:, 4 + tt % 2, k * P:(k + 1) * P], tn[:, tt % 2, k * P:(k + 1) * P], ident[:])
                    last.then_inc(tr_mm[L], 1)

            pe.wait_ge(xn_ok[2], TT)
            for tt in range(TT):
                for k in range(KT):
                    last = mm(ps[:, 6, tt * NE:(tt + 1) * NE], xnT[:, k, tt * P:(tt + 1) * P], gate[:, k, :],
                              start=(k == 0), stop=(k == KT - 1))
            last.then_inc(lg_mm, 1)
            pe.wait_ge(lg_ev, 1)
            n = 0
            for e in range(NE):
                pe.wait_ge(ld_1[e % 2], 32 * (e // 2 + 1))
                for half in range(2):
                    def hidden(c):
                        for k in range(KT):
                            last = mm(ps[:, c % 4, :], w1[e % 2][:, k, c * P:(c + 1) * P],
                                      xnT[:, k, half * HALF:(half + 1) * HALF], start=(k == 0), stop=(k == KT - 1))
                        last.then_inc(h_mm, 1)

                    def output(c):
                        for j in range(4):
                            if c == 0:
                                wait(pe, y_ev, 4 * (2 * e + half) - 4 + j + 1 if e + half else 0)
                                mm(ps[:, 4 + j, 0:C], ones[0:1, :], b2[0:1, e, :], start=True, stop=False)
                            last = mm(ps[:, 4 + j, 0:C], hT[:, c % 4, j * P:(j + 1) * P], w2[e % 2][:, c, :],
                                      start=False, stop=(c == HC - 1))
                        return last
                    base = HC * (2 * e + half)
                    for c in range(HC + 2):
                        if c < HC:
                            wait(pe, h_ev, base + c - 3)
                            hidden(c)
                        if c >= 2:
                            pe.wait_ge(h_ev, base + c - 1)
                            last = output(c - 2)
                    last.then_inc(y_mm, 1)

        @block.vector
        def _(v):
            done = [0]

            def own(ins):
                done[0] += 1
                ins.then_inc(dv, 1)
                v.wait_ge(dv, done[0])

            own(v.memset(bd[:], 0.0))
            for i in L2:
                v.memset(va[i][:, :, HD:2 * HD], 1.0)
                v.memset(f(ka[i][96:104, :]), 1.0)
            v.memset(ones[:], 1.0).then_inc(consts, 2)
            v.wait_ge(ld_c, 16 * 5)
            v.wait_ge(ld_c, 16 * 21)
            v.tensor_copy(eb[:], ebf).then_inc(consts, 1)
            for g in range(4):
                rows = slice(g * HD, (g + 1) * HD)
                v.tensor_copy(bd[rows, :, :, g], tab[rows]).then_inc(bd_ok, 1)
            v.wait_ge(ld_x, 48)
            for k in range(KT):
                for half in range(2):
                    own(v.bn_stats(stat[:, k, 6 * half:6 * half + 6], xnT[:, k, half * HALF:(half + 1) * HALF]))
                last = v.bn_aggr(mv[:, k, :], stat[:, k, :])
                own(last)
            v.sem_inc(consts, 1)
            v.wait_ge(g_sum, 1)
            own(v.tensor_copy(gm[:, :, 0], ps[:, 0, 0:KT]))
            own(v.tensor_tensor(gd[:], mv[:, 0:KT, 0], gm[:, :, 0], ALU.subtract))
            own(v.tensor_tensor(gd[:], gd[:], gd[:], ALU.mult))
            own(v.tensor_tensor(gd[:], gd[:], mv[:, 0:KT, 1], ALU.add))
            v.sem_inc(consts, 1)
            v.wait_ge(g_sum, 2)
            v.tensor_scalar(gm[:, :, 1], ps[:, 1, 0:KT], 1e-5, None, ALU.add).then_inc(lx, 1)
            v.wait_ge(av, 1)
            own(v.reciprocal(rstd[:, 0:KT], sd[:, 0:KT]))
            for k in range(KT):
                v.tensor_scalar(xnT[:, k, :], xnT[:, k, :], gm[:, k, 0:1], rstd[:, k:k + 1],
                                ALU.subtract, ALU.mult).then_inc(xn_ok[0], 1)

            for L in L2:
                n = 0
                for u in range(2 * KT):
                    src = qf[:, u, :] if u < KT else kf[:, u % 2, :]
                    s = SCALE[L] if u < KT else 1.0
                    v.wait_ge(qk_ev[L], u + 1)
                    hi, lo = stage[:, n % 4, :], stage[:, (n + 1) % 4, :]
                    wait(v, st_s[L][n % 4], stored(n))
                    wait(v, st_s[L][(n + 1) % 4], stored(n + 1))
                    ins = v.tensor_scalar(hi, src, s, None, ALU.mult).then_inc(split[L], 1)
                    v.wait_ge(split[L], n + 1)
                    v.scalar_tensor_tensor(lo, src, s, f(hi), ALU.mult, ALU.subtract).then_inc(split[L], 1)
                    n += 2
                for tt in range(TT):
                    v.wait_ge(v_mm[L], tt + 1)
                    if L == 0:
                        v.tensor_tensor(vf[:, tt, :], ps[:, 4 + tt % 4, 0:C], bv[:], ALU.add).then_inc(v_ev[L], 1)
                    else:
                        v.tensor_copy(vf[:, tt, :], ps[:, 4 + tt % 4, 0:C]).then_inc(v_ev[L], 1)
                if L == 0:
                    rel = prob[:, 0:KT, :]
                    for w in range(2):
                        view = rel.rearrange("p g (h w) -> p g h w", w=SIDE)
                        for i in range(SIDE // 4):
                            v.wait_ge(rel_mm, 8 * w + i + 1)
                            if w == 1 and i == 0:
                                v.wait_ge(split[L], n)
                            for g in range(KT):
                                src = ps[:, (8 * w + i) % 4, 0:C].rearrange("p (j g x) -> p g j x", j=4, g=KT)[:, g]
                                dst = view[:, g, 4 * i:4 * i + 4, :] if w == 0 else \
                                    view[:, g, :, 4 * i:4 * i + 4].rearrange("p h j -> p j h")
                                ins = v.tensor_copy(dst, src)
                            ins.then_inc(rel_ev, 1)
                        v.wait_ge(rel_ev, 8 * w + 8)
                        for g in range(KT):
                            hi, lo = stage[:, n % 4, :], stage[:, (n + 1) % 4, :]
                            wait(v, st_s[L][n % 4], stored(n))
                            wait(v, st_s[L][(n + 1) % 4], stored(n + 1))
                            v.tensor_copy(hi, rel[:, g, :]).then_inc(split[L], 1)
                            v.wait_ge(split[L], n + 1)
                            v.tensor_tensor(lo, rel[:, g, :], f(hi), ALU.subtract).then_inc(split[L], 1)
                            n += 2
                v.wait_ge(split[L], n)

                def maximum(h, b, qt):
                    v.wait_ge(sm_ok[L], TT * h + qt + 1)
                    if qt == 0:
                        wait(v, mT_ok[L], h - 1)
                    v.tensor_reduce(mcol[:, b, qt:qt + 1], ps[:, 0:2, :], AX.XY, ALU.max).then_inc(mx_ok[L], 1)

                def place_max(h, b):
                    v.wait_ge(mT_ok[L], h + 1)
                    wait(v, st_ok[L], TT * (h - 1))
                    v.tensor_tensor(qa[b][96:104, :].rearrange("p (t q) -> p t q", q=P),
                                    ps[0:TT, 6 + b, 0:P].unsqueeze(1).broadcast_to([TT, TT, P]),
                                    negd[:], ALU.mult).then_inc(r_ok[L], 1)

                def evacuate(h, b, half):
                    v.wait_ge(pv_ok[L], TT * (h + 1))
                    wait(v, st_o[L][b], 8 * (h - b))
                    wait(v, o_ok[L], 2 * h + half)
                    v.reciprocal(rec[:], ps[64 * half + 32:64 * half + 64, 6 + b, :]).then_inc(o_rc[L], 1)
                    v.wait_ge(o_rc[L], 2 * h + half + 1)
                    v.tensor_tensor(osb[b][:, half * HALF:(half + 1) * HALF], ps[64 * half:64 * half + 32, 6 + b, :],
                                    rec[:], ALU.mult).then_inc(o_ok[L], 1)

                def head(h, b, first=False, left=2):
                    for s in range(TT):
                        if s < 6 and left >= 1:
                            maximum(h + 1, 1 - b, s + 2)
                        if s == 7 and left >= 1:
                            place_max(h + 1, 1 - b)
                        if s >= 6 and left >= 2:
                            maximum(h + 2, b, s - 6)
                        if s in (1, 2) and not first:
                            evacuate(h - 1, 1 - b, s - 1)

                for m in range(TT):
                    maximum(0, 0, m)
                place_max(0, 0)
                maximum(1, 1, 0)
                maximum(1, 1, 1)
                head(0, 0, first=True)
                head(1, 1)
                with v.Fori(1, NH // 2 - 1) as i:
                    head(2 * i, 0)
                    head(2 * i + 1, 1)
                head(NH - 2, 0, left=1)
                head(NH - 1, 1, left=0)
                evacuate(NH - 1, 1, 0)
                evacuate(NH - 1, 1, 1)

                own(v.tensor_tensor(t[:], t[:], bproj[:, L:L + 1, :].broadcast_to([P, TT, C]), ALU.add))
                for tt in range(TT):
                    v.wait_ge(pj_mm[L], tt + 1)
                    v.tensor_tensor(t[:, tt, :], t[:, tt, :], ps[:, tt % 4, 0:C], ALU.add).then_inc(t_ok[L], 1)
                    v.wait_ge(t_ok[L], tt + 1)
                    own(v.bn_stats(stat[:, tt, 0:6], t[:, tt, :]))
                    own(v.bn_aggr(mv[:, tt, :], stat[:, tt, 0:6]))
                v.tensor_scalar(m8[:], mv[:, :, 1], 1e-5, None, ALU.add).then_inc(lx, 1)
                v.wait_ge(av, 2 + L)
                own(v.reciprocal(rstd[:], sd[:]))
                for tt in range(TT):
                    wait(v, tr_mm[L], tt - 1)
                    v.tensor_scalar(tn[:, tt % 2, :], t[:, tt, :], mv[:, tt, 0:1], rstd[:, tt:tt + 1],
                                    ALU.subtract, ALU.mult).then_inc(tn_ok[L], 1)

            v.wait_ge(lg_mm, 1)
            own(v.tensor_tensor(lg[:], ps[:, 6, 0:TT * NE].rearrange("p (t e) -> p t e", e=NE),
                                gateb[:].unsqueeze(1).broadcast_to([P, TT, NE]), ALU.add))
            v.sem_inc(lg_ev, 1)
            own(v.tensor_reduce(m8[:], lg[:], AX.X, ALU.max))
            v.tensor_tensor(lg[:], lg[:], m8[:].unsqueeze(2).broadcast_to([P, TT, NE]), ALU.subtract).then_inc(lx, 1)
            v.wait_ge(av, 4)
            own(v.tensor_reduce(s8[:], pr[:], AX.X, ALU.add))
            own(v.reciprocal(s8[:], s8[:]))
            own(v.tensor_tensor(pr[:], pr[:], s8[:].unsqueeze(2).broadcast_to([P, TT, NE]), ALU.mult))
            mine = pr[:].unsqueeze(3).broadcast_to([P, TT, NE, NE])
            other = pr[:].unsqueeze(2).broadcast_to([P, TT, NE, NE])
            own(v.tensor_tensor(cm[:], other, mine, ALU.is_gt))
            own(v.tensor_tensor(cm2[:], other, mine, ALU.is_equal))
            own(v.tensor_tensor(cm2[:], cm2[:], low[:].unsqueeze(1).broadcast_to([P, TT, NE, NE]), ALU.mult))
            own(v.tensor_tensor(cm[:], cm[:], cm2[:], ALU.add))
            own(v.tensor_reduce(rk[:], cm[:], AX.X, ALU.add))
            own(v.scalar_tensor_tensor(w8[:], rk[:], 1.5, pr[:], ALU.is_lt, ALU.mult))
            own(v.tensor_reduce(s8[:], w8[:], AX.X, ALU.add))
            own(v.reciprocal(s8[:], s8[:]))
            own(v.tensor_tensor(w8[:], w8[:], s8[:].unsqueeze(2).broadcast_to([P, TT, NE]), ALU.mult))
            for e in range(NE):
                for half in range(2):
                    v.wait_ge(y_mm, 2 * e + half + 1)
                    for j in range(4):
                        tt = 4 * half + j
                        if e:
                            v.wait_ge(y_ev, 8 * (e - 1) + tt + 1)
                        v.scalar_tensor_tensor(t[:, tt, :], ps[:, 4 + j, 0:C], w8[:, tt, e:e + 1], t[:, tt, :],
                                               ALU.mult, ALU.add).then_inc(y_ev, 1)

        @block.scalar
        def _(act):
            act.wait_ge(lx, 1)
            act.activation(sd[:, 0:KT], gm[:, :, 1], ACT.Sqrt).then_inc(av, 1)
            for L in L2:
                for u in range(2 * KT):
                    act.wait_ge(qk_mm[L], u + 1)
                    if u >= KT + 2:
                        act.wait_ge(split[L], 2 * (u - 1))
                    dst = qf[:, u, :] if u < KT else kf[:, u % 2, :]
                    src = ps[:, 2 * (u % 2):2 * (u % 2) + 2, :].rearrange("p a b -> p (a b)")
                    if L == 0:
                        act.activation(dst, src, ACT.Identity, bias=bqk[:, u:u + 1]).then_inc(qk_ev[L], 1)
                    else:
                        act.activation(dst, src, ACT.Copy).then_inc(qk_ev[L], 1)
                if L == 0:
                    act.wait_ge(split[0], 24)

                def head(h, b, first=False):
                    for s in range(TT):
                        act.wait_ge(st_ok[L], TT * h + s + 1)
                        wait(act, pv_ok[L], TT * h + s + 1 - NP)
                        act.activation(prob[:, s % NP, :], ps[:, 2 + 2 * (s % 2):4 + 2 * (s % 2), :].rearrange("p a b -> p (a b)"),
                                       ACT.Exp).then_inc(p_ok[L], 1)
                        if s == 5 and not first:
                            store(h - 1, 1 - b)

                def store(h, b):
                    rows = hrow(act, h)
                    act.wait_ge(o_ok[L], 2 * (h + 1))
                    act.dma_start(att_dram[L][rows, :], osb[b][:]).then_inc(st_o[L][b], 16)

                head(0, 0, first=True)
                head(1, 1)
                with act.Fori(1, NH // 2 - 1) as i:
                    head(2 * i, 0)
                    head(2 * i + 1, 1)
                head(NH - 2, 0)
                head(NH - 1, 1)
                store(NH - 1, 1)
                act.wait_ge(lx, 2 + L)
                act.activation(sd[:], m8[:], ACT.Sqrt).then_inc(av, 1)
                for tt in range(TT):
                    act.wait_ge(tr_mm[L], tt + 1)
                    act.activation(xnT[:, :, tt * P:(tt + 1) * P],
                                   ps[:, 4 + tt % 2, 0:C].rearrange("p (k q) -> p k q", k=KT), ACT.Copy).then_inc(xn_ok[L + 1], 1)
            act.wait_ge(lx, 4)
            act.activation(pr[:], lg[:], ACT.Exp).then_inc(av, 1)
            for n in range(2 * NE * HC):
                e, c = n // (2 * HC), n % HC
                act.wait_ge(h_mm, n + 1)
                act.activation(hT[:, c % 4, :], ps[:, c % 4, :], ACT.Relu, bias=b1[:, e, c:c + 1]).then_inc(h_ev, 1)


def constants():
    key = np.arange(N)
    rows = np.arange(SIDE)[:, None]
    pos = np.concatenate([key // SIDE == rows, key % SIDE == rows])
    group = np.arange(C) // GROUP
    same = (group[:, None] == group[None, :]) / np.float32(GROUP)
    blocks = same.reshape(KT, P, KT, P).transpose(0, 2, 1, 3).reshape(KT * KT, P, P)
    negd = np.zeros((TT, TT, P), np.float32)
    for i in range(TT):
        negd[i, i] = -1.0
    low = np.broadcast_to(np.tril(np.ones((NE, NE)), -1), (P, NE, NE))
    return {
        "ident": np.eye(P, dtype=np.float32), "grp": blocks.astype(np.float32),
        "eb": np.concatenate([pos, pos]).astype(np.float32), "negd": negd,
        "low": np.ascontiguousarray(low, np.float32),
    }


def kernel(x, L0_conv_qkv_w, L0_conv_qkv_b, L0_conv_proj_w, L0_conv_proj_b, L0_conv_rel_pos_h, L0_conv_rel_pos_w,
           L1_attn_w_qkv, L1_attn_w_proj, L1_attn_b_proj, L1_ffn_gate_w, L1_ffn_gate_b, L1_ffn_w1, L1_ffn_b1,
           L1_ffn_w2, L1_ffn_b2):
    import concourse.bacc as bacc
    from concourse.bass_utils import run_bass_kernel_spmd as run

    tokens = np.asarray(x).reshape(N, C)
    arrays = {
        "x": tokens, "xT": tokens.T,
        "wqkv0": np.asarray(L0_conv_qkv_w).T, "wqkv1": np.asarray(L1_attn_w_qkv).T,
        "bqk": np.asarray(L0_conv_qkv_b)[:2 * C].reshape(2 * KT, P).T, "bv": np.asarray(L0_conv_qkv_b)[2 * C:],
        "wproj0": np.asarray(L0_conv_proj_w).T, "bproj0": np.asarray(L0_conv_proj_b),
        "wproj1": np.asarray(L1_attn_w_proj).T, "bproj1": np.asarray(L1_attn_b_proj),
        "relh": np.asarray(L0_conv_rel_pos_h)[::-1].T, "relw": np.asarray(L0_conv_rel_pos_w)[::-1].T,
        "gate": np.asarray(L1_ffn_gate_w).T, "gateb": np.asarray(L1_ffn_gate_b),
        "w1": np.asarray(L1_ffn_w1).transpose(0, 2, 1), "b1": np.asarray(L1_ffn_b1).reshape(NE, HC, P).transpose(2, 0, 1),
        "w2": np.asarray(L1_ffn_w2).transpose(0, 2, 1), "b2": np.asarray(L1_ffn_b2),
    }
    arrays.update(constants())
    arrays = {k: np.ascontiguousarray(v) for k, v in arrays.items()}
    nc = bacc.Bacc("TRN2", target_bir_lowering=False, num_devices=1)
    aps = {k: nc.dram_tensor(f"in_{k}", v.shape, mybir.dt.from_np(v.dtype), kind="ExternalInput").ap()
           for k, v in arrays.items()}
    aps["out"] = nc.dram_tensor("out_0", (N, C), F32, kind="ExternalOutput").ap()
    build_program(nc, aps)
    result = run(nc, [{f"in_{k}": v for k, v in arrays.items()}], core_ids=[0])
    return np.asarray(result.results[0]["out_0"]).reshape(np.shape(x))
```

```python
from contextlib import ExitStack

import numpy as np
import concourse.bass as bass
from concourse import mybir

F32 = mybir.dt.float32
F32R = mybir.dt.float32r
I32 = mybir.dt.int32
U32 = mybir.dt.uint32
ALU = mybir.AluOpType
ACT = mybir.ActivationFunctionType
AX = mybir.AxisListType

P = 128
C = 384
KT = C // P
SIDE = 32
N = SIDE * SIDE
TT = N // P
NH = 12
HD = C // NH
HALF = 512
NE = 8
HID = 4 * C
HC = HID // P
GROUP = C // 32
REL = 2 * SIDE - 1
SCALE = (HD ** -0.5, C ** -0.5)
NP = 4
WQ = 3
WN = HID // WQ
WC = HC // WQ
TILES = 2 * TT + NE - 1
SLOTS = (TILES + 1) * P

Q_LO, Q_HI, RH_HI, RW_HI, RH_LO, RW_LO, K_HI, K_LO = range(8)


def build_program(nc, a):
    ctx = ExitStack()
    with ctx:
        def sem(name):
            return ctx.enter_context(nc.semaphore(name))

        def sb(name, shape, dt=F32, where=ctx):
            return where.enter_context(nc.sbuf_tensor(name, shape, dt))

        ps = ctx.enter_context(nc.psum_tensor("ps", [P, 8, HALF], F32))

        heads_dram = [nc.dram_tensor(f"heads{L}", [8, C, N], F32).ap() for L in range(2)]
        v_dram = [nc.dram_tensor(f"v{L}", [NH, P, TT, HD], F32).ap() for L in range(2)]
        att_dram = [nc.dram_tensor(f"att{L}", [C, N], F32).ap() for L in range(2)]

        xs_dram = nc.dram_tensor("xs", [SLOTS, C], F32).ap()
        ys_dram = nc.dram_tensor("ys", [SLOTS, C], F32).ap()

        t = sb("t", [P, TT, C])
        xnT = sb("xnT", [P, KT, N])
        ident = sb("ident", [P, P])
        before = sb("before", [P, P])
        ones = sb("ones", [P, P])
        bqk = sb("bqk", [P, 6])
        bv = sb("bv", [P, C])
        bproj = sb("bproj", [P, 2, C])
        gate = sb("gate", [P, KT, NE])
        gateb = sb("gateb", [P, NE])
        stat = sb("stat", [P, TT, 12])
        mv = sb("mv", [P, TT, 2])
        sd = sb("sd", [P, TT])
        rstd = sb("rstd", [P, TT])
        gm = sb("gm", [P, KT, 2])
        gd = sb("gd", [P, KT])
        zero = sb("zero", [P, C])

        def placed(start):
            at = [start]

            def put(name, shape, dt=F32):
                tensor = nc.alloc_sbuf_tensor_at(name, shape, dt, offset=at[0])
                at[0] += -(-int(np.prod(shape[1:])) * 4 // 32) * 32
                return tensor
            return put, at

        first_start = -(-nc.sbuf_base // 32) * 32
        put, first_end = placed(first_start)
        w1_raw0, w2_raw0 = put("w1_raw0", [P, KT, HID]), put("w2_raw0", [P, HC, C])
        low0, _ = placed(first_start)
        start = first_end[0]
        put, att_end = placed(start)
        vf = put("vf", [P, TT, C])
        oT = vf[:, :, :].rearrange("p a b -> p (a b)").rearrange("p (k n) -> p k n", k=KT)
        wproj = put("wproj", [P, KT, C])
        wqkv = put("wqkv", [P, KT, 3 * C])
        eb = put("eb", [P, N], F32R)
        qa = [put(f"qa{i}", [104, N], F32R) for i in range(2)]
        ka = [put(f"ka{i}", [104, N], F32R) for i in range(2)]
        qm = [put(f"qm{i}", [96, N], F32R) for i in range(2)]
        km = [put(f"km{i}", [96, N], F32R) for i in range(2)]
        qb = [put(f"qb{i}", [P, N], F32R) for i in range(2)]
        va = [put(f"va{i}", [P, TT, HD]) for i in range(2)]
        prob = put("prob", [P, NP, N])
        qf = put("qf", [P, KT, N])
        stage = put("stage", [P, 4, N], F32R)
        bd = put("bd", [P, 2, REL, 4])
        tab = put("tab", [P, 2, REL])
        mcol = put("mcol", [P, 2, TT])
        negd = put("negd", [TT, TT, P])
        kf = prob[:, 0:2, :]
        ebf = prob[:, 3, :]
        grp = qf[:, 0, :].rearrange("p (a b) -> p a b", b=P)
        osb = [stage[0:2 * HD, i, 0:HALF].bitcast(F32) for i in range(2)]
        rec = stage[0:2 * HD, 2, 0:HALF].bitcast(F32)
        raw, raw_end = placed(start)
        low_put, _ = placed(start)
        w1_raw = [w1_raw0, raw("w1_raw1", [P, KT, HID])]
        w2_raw = [w2_raw0, raw("w2_raw1", [P, HC, C])]
        w1_lo = [low0("w1_lo0", [P, KT, HID], F32R), low_put("w1_lo1", [P, KT, HID], F32R)]
        w2_lo = [low0("w2_lo0", [P, HC, C], F32R), low_put("w2_lo1", [P, HC, C], F32R)]
        put, moe_end = placed(raw_end[0])
        w1_hi = [None, put("w1_hi1", [P, KT, HID], F32R)]
        w2_hi = [None, put("w2_hi1", [P, HC, C], F32R)]
        gather_put, _ = placed(moe_end[0])
        w1_hi[0] = put("w1_hi0", [P, KT, HID], F32R)
        w2_hi[0] = put("w2_hi0", [P, HC, C], F32R)
        gy = gather_put("gy", [P, 2, TT, C])
        tn_put, _ = placed(moe_end[0])
        h_hi = put("h_hi", [P, HC, P], F32R)
        h_lo = put("h_lo", [P, HC, P], F32R)
        tn = tn_put("tn", [P, TT, C])
        gate_put, _ = placed(moe_end[0])
        cm = gate_put("cm", [P, TT, NE, NE])
        cm2 = gate_put("cm2", [P, TT, NE, NE])
        h_b = put("h_b", [P, 2, 2, P])
        h_sum = put("h_sum", [P, 2, 2, P])
        xs = put("xs", [P, C])
        x2 = put("x2", [P, KT, 2, P], F32R)
        ysb = put("ysb", [P, C])
        b1c = [put(f"b1c{i}", [P, HC]) for i in range(2)]
        b2c = [put(f"b2c{i}", [P, C]) for i in range(2)]
        lg = put("lg", [P, TT, NE])
        pr = put("pr", [P, TT, NE])
        w8 = put("w8", [P, TT, NE])
        rk = put("rk", [P, TT, NE])
        first = put("first", [P, NE, NE])
        above = put("above", [P, NE, NE])
        m8 = put("m8", [P, TT])
        s8 = put("s8", [P, TT])
        taken = put("taken", [P, TT + 1, NE])
        choice = put("choice", [P, 2, TT, NE])
        prod = put("prod", [P, 2, TT, NE])
        ntile = put("ntile", [P, NE])
        cum = put("cum", [P, NE + 1])
        cum_i = put("cum_i", [P, NE + 1], I32)
        slot = put("slot", [P, TT, NE])
        where = put("where", [P, 2, TT])
        where_i = put("where_i", [P, 2, TT], U32)
        wts = put("wts", [P, 2, TT])
        assert max(att_end[0], moe_end[0]) <= nc.sbuf_top, (att_end, moe_end)

        ld_x = sem("ld_x")
        ld_c = sem("ld_c")
        ld_w = [sem(f"ld_w{L}") for L in range(2)]
        ld_e = sem("ld_e")
        consts = sem("consts")
        bd_ok = sem("bd_ok")
        m_free = sem("m_free")
        a_free = sem("a_free")
        dv = sem("dv")
        av = sem("av")
        g_sum = sem("g_sum")
        xn_ok = [sem(f"xn_ok{L}") for L in range(3)]
        L2 = range(2)
        qk_mm = [sem(f"qk_mm{L}") for L in L2]
        qk_ev = [sem(f"qk_ev{L}") for L in L2]
        v_mm = [sem(f"v_mm{L}") for L in L2]
        v_ev = [sem(f"v_ev{L}") for L in L2]
        split = [sem(f"split{L}") for L in L2]
        st_v = [sem(f"st_v{L}") for L in L2]
        st_s = [[sem(f"st_s{L}_{i}") for i in range(4)] for L in L2]
        rel_mm = sem("rel_mm")
        rel_hi = sem("rel_hi")
        rel_ev = sem("rel_ev")
        ld_m = [[sem(f"ld_m{L}{i}") for i in L2] for L in L2]
        ld_a = [[sem(f"ld_a{L}{i}") for i in L2] for L in L2]
        sm_ok = [sem(f"sm_ok{L}") for L in L2]
        mx_ok = [sem(f"mx_ok{L}") for L in L2]
        mT_ok = [sem(f"mT_ok{L}") for L in L2]
        r_ok = [sem(f"r_ok{L}") for L in L2]
        st_ok = [sem(f"st_ok{L}") for L in L2]
        p_ok = [sem(f"p_ok{L}") for L in L2]
        pv_ok = [sem(f"pv_ok{L}") for L in L2]
        o_rc = [sem(f"o_rc{L}") for L in L2]
        o_ok = [sem(f"o_ok{L}") for L in L2]
        st_o = [[sem(f"st_o{L}{i}") for i in L2] for L in L2]
        ld_o = [sem(f"ld_o{L}") for L in L2]
        pj_mm = [sem(f"pj_mm{L}") for L in L2]
        t_ok = [sem(f"t_ok{L}") for L in L2]
        tn_ok = [sem(f"tn_ok{L}") for L in L2]
        tr_mm = [sem(f"tr_mm{L}") for L in L2]
        lg_mm = sem("lg_mm")
        lg_ev = sem("lg_ev")
        lx = sem("lx")
        ld_g = sem("ld_g")
        w_hi = sem("w_hi")
        w8_ok = sem("w8_ok")
        zero_st = sem("zero_st")
        sel_ok = sem("sel_ok")
        cnt_mm = sem("cnt_mm")
        cum_ok = sem("cum_ok")
        where_ok = sem("where_ok")
        scattered = sem("scattered")
        ld_1 = [[sem(f"ld_1{i}_{q}") for q in range(2 * WQ)] for i in L2]
        ld_b = [sem(f"ld_b{i}") for i in L2]
        w_ok = [sem(f"w_ok{i}") for i in L2]
        x_ld = sem("x_ld")
        x_mm = sem("x_mm")
        x_hi = sem("x_hi")
        x_lo = sem("x_lo")
        h_mm = sem("h_mm")
        h_b_ok = sem("h_b_ok")
        h_s_ok = sem("h_s_ok")
        h_h_ok = sem("h_h_ok")
        h_l_ok = sem("h_l_ok")
        y_mm = sem("y_mm")
        y_ev = sem("y_ev")
        y_st = sem("y_st")
        y_all = sem("y_all")
        gathered = [sem(f"gathered{i}") for i in range(TT)]
        t_out = sem("t_out")
        out_st = sem("out_st")

        def wait(eng, s, value):
            if not isinstance(value, int) or value > 0:
                eng.wait_ge(s, value)

        def stored(n):
            return 16 * sum(1 if i < 4 * KT else 4 for i in range(n % 4, n, 4))

        def f(ap):
            return ap.bitcast(F32)

        def piece1(w, q):
            return w[:, :, q * WN:(q + 1) * WN]

        def piece2(w, q):
            return w[:, q * WC:(q + 1) * WC, :]

        def hrow(eng, h):
            return bass.ds(h * HD if isinstance(h, int) else eng.snap(h * HD), HD)

        block = ctx.enter_context(nc.Block())

        @block.sync
        def _(sp):
            sp.dma_start(xnT[:], a["xT"].rearrange("(k p) n -> p k n", p=P)).then_inc(ld_x, 16)
            sp.dma_start(grp, a["grp"].rearrange("g p c -> p g c")[:, 0:8, :]).then_inc(ld_x, 16)
            sp.dma_start(qf[:, 1, 0:P], a["grp"][8]).then_inc(ld_x, 16)
            sp.dma_start(wqkv[:], a["wqkv0"].rearrange("(k p) n -> p k n", p=P)).then_inc(ld_w[0], 16)
            for dst, name in ((ident[:], "ident"), (bqk[:], "bqk"), (negd[:], "negd"), (ebf, "eb")):
                sp.dma_start(dst, a[name]).then_inc(ld_c, 16)
            for dst, name in ((bv[:], "bv"), (bproj[:, 0, :], "bproj0"), (bproj[:, 1, :], "bproj1"),
                              (gateb[:], "gateb")):
                sp.dma_start(dst, a[name].partition_broadcast(P)).then_inc(ld_c, 16)
            sp.dma_start(t[:], a["x"].rearrange("(t p) c -> p t c", p=P)).then_inc(ld_c, 16)
            sp.dma_start(before[:], a["before"]).then_inc(ld_c, 16)
            sp.dma_start(gate[:], a["gate"].rearrange("(k p) e -> p k e", p=P)).then_inc(ld_c, 16)
            for i, name in enumerate(("relh", "relw")):
                for g in range(4):
                    sp.dma_start(tab[g * HD:(g + 1) * HD, i, :], a[name]).then_inc(ld_c, 16)
            sp.wait_ge(consts, 3)
            for i in L2:
                sp.dma_start(f(km[i][32:96, :]), f(eb[0:64, :])).then_inc(ld_e, 16)

            def load_expert(e):
                b = e % 2
                for q in range(WQ):
                    sp.dma_start(piece1(w1_raw[b], q), a["w1"][e].rearrange("(k p) n -> p k n", p=P)[:, :, q * WN:(q + 1) * WN]).then_inc(ld_1[b][q], 16)
                for q in range(WQ):
                    sp.dma_start(piece2(w2_raw[b], q), a["w2"][e].rearrange("(k p) n -> p k n", p=P)[:, q * WC:(q + 1) * WC, :]).then_inc(ld_1[b][WQ + q], 16)

            for L in L2:
                if L == 0:
                    sp.wait_ge(consts, 2)
                    for i in range(TILES + 1):
                        sp.dma_start(xs_dram[i * P:(i + 1) * P, :], zero[:]).then_inc(zero_st, 16)
                    for i in range(2 * TT, TILES + 1):
                        sp.dma_start(ys_dram[i * P:(i + 1) * P, :], zero[:]).then_inc(zero_st, 16)
                order = []
                for m in range(KT):
                    order += [(Q_HI, m), (Q_LO, m)]
                for m in range(KT):
                    order += [(K_HI, m), (K_LO, m)]
                if L == 0:
                    for hi, lo in ((RH_HI, RH_LO), (RW_HI, RW_LO)):
                        for m in range(KT):
                            order += [(hi, m), (lo, m)]
                for n, (slot, m) in enumerate(order):
                    sp.wait_ge(split[L], n + 1)
                    dst, src = heads_dram[L][slot, m * P:(m + 1) * P, :], f(stage[:, n % 4, :])
                    if slot in (RH_HI, RW_HI, RH_LO, RW_LO):
                        for g in range(4):
                            sp.dma_start(dst[g * HD:(g + 1) * HD, :], src[g:P:4, :]).then_inc(st_s[L][n % 4], 16)
                    else:
                        sp.dma_start(dst, src).then_inc(st_s[L][n % 4], 16)
                sp.wait_ge(v_ev[L], TT)
                for h in range(NH):
                    sp.dma_start(v_dram[L][h], vf[:, :, h * HD:(h + 1) * HD]).then_inc(st_v[L], 16)
                for i in range(4):
                    sp.wait_ge(st_s[L][i], stored(len(order) + i))
                sp.wait_ge(st_v[L], 16 * NH)
                H = heads_dram[L]

                def load_m(h, b):
                    rows = hrow(sp, h)
                    wait(sp, sm_ok[L], TT * (h - 1))
                    sp.sem_inc(m_free, 1)
                    sp.dma_start(f(qm[b][0:32, :]), H[Q_HI, rows, :]).then_inc(ld_m[L][b], 16)
                    sp.dma_start(f(km[b][0:32, :]), H[K_HI, rows, :]).then_inc(ld_m[L][b], 16)
                    if L == 0:
                        sp.dma_start(f(qm[b][32:64, :]), H[RH_HI, rows, :]).then_inc(ld_m[L][b], 16)
                        sp.dma_start(f(qm[b][64:96, :]), H[RW_HI, rows, :]).then_inc(ld_m[L][b], 16)

                def load_a(h, b):
                    rows = hrow(sp, h)
                    wait(sp, pv_ok[L], TT * (h - 1))
                    sp.sem_inc(a_free, 1)
                    for i, slot in enumerate((Q_LO, Q_HI, Q_HI)):
                        sp.dma_start(f(qa[b][32 * i:32 * i + 32, :]), H[slot, rows, :]).then_inc(ld_a[L][b], 16)
                    for i, slot in enumerate((K_HI, K_HI, K_LO)):
                        sp.dma_start(f(ka[b][32 * i:32 * i + 32, :]), H[slot, rows, :]).then_inc(ld_a[L][b], 16)
                    if L == 0:
                        for i, slot in enumerate((RH_HI, RW_HI, RH_LO, RW_LO)):
                            sp.dma_start(f(qb[b][32 * i:32 * i + 32, :]), H[slot, rows, :]).then_inc(ld_a[L][b], 16)
                    sp.dma_start(va[b][:], v_dram[L][bass.ds(h, 1)].rearrange("h p t d -> p (h t) d")).then_inc(ld_a[L][b], 16)

                if L == 1:
                    sp.wait_ge(pv_ok[0], TT * NH)
                load_m(0, 0)
                load_a(0, 0)
                load_m(1, 1)
                load_a(1, 1)
                load_m(2, 0)
                load_a(2, 0)
                load_m(3, 1)
                with sp.Fori(1, NH // 2 - 1) as i:
                    load_a(2 * i + 1, 1)
                    load_m(2 * i + 2, 0)
                    load_a(2 * i + 2, 0)
                    load_m(2 * i + 3, 1)
                load_a(NH - 1, 1)
                if L == 0:
                    sp.dma_start(wproj[:], a["wproj0"].rearrange("(k p) n -> p k n", p=P)).then_inc(ld_w[0], 16)
                    sp.wait_ge(v_mm[0], TT)
                    sp.dma_start(wqkv[:], a["wqkv1"].rearrange("(k p) n -> p k n", p=P)).then_inc(ld_w[1], 16)
                else:
                    load_expert(0)
                    sp.wait_ge(pj_mm[0], TT)
                    sp.dma_start(wproj[:], a["wproj1"].rearrange("(k p) n -> p k n", p=P)).then_inc(ld_w[1], 16)
                for i in L2:
                    sp.wait_ge(st_o[L][i], 16 * NH)
                sp.dma_start(oT, att_dram[L].rearrange("(k p) n -> p k n", p=P)).then_inc(ld_o[L], 16)

            def load_biases(e):
                b = e % 2
                sp.dma_start(b1c[b][:], a["b1"][e]).then_inc(ld_b[b], 16)
                sp.dma_start(b2c[b][:], a["b2"][e].partition_broadcast(P)).then_inc(ld_b[b], 16)

            sp.wait_ge(pj_mm[1], TT)
            load_expert(1)
            load_biases(0)
            load_biases(1)
            for dst, name in ((first[:], "low"), (above[:], "above")):
                sp.dma_start(dst, a[name]).then_inc(ld_g, 16)
            sp.wait_ge(scattered, 16 * 2 * TT)
            sp.dma_start(xs[:], xs_dram[0:P, :]).then_inc(x_ld, 16)
            sp.wait_ge(cum_ok, 1)
            for e in range(NE):
                begin = sp.value_load(cum_i[0:1, e:e + 1], min_val=e, max_val=TILES)
                end = sp.value_load(cum_i[0:1, e + 1:e + 2], min_val=e + 1, max_val=TILES)
                if 1 <= e < NE - 1:
                    sp.wait_ge(y_ev, begin + 1)
                    load_expert(e + 1)
                    load_biases(e + 1)
                with sp.Fori(begin, end) as j:
                    ahead = sp.snap(j * P + P)
                    here = sp.snap(j * P)
                    sp.wait_ge(x_mm, j + 1)
                    sp.dma_start(xs[:], xs_dram[bass.ds(ahead, P), :]).then_inc(x_ld, 16)
                    sp.wait_ge(y_ev, j + 2)
                    sp.dma_start(ys_dram[bass.ds(here, P), :], ysb[:]).then_inc(y_st, 16)
            sp.wait_ge(y_st, end * 16 + 16)
            sp.sem_inc(y_all, 1)
            for tt in range(TT):
                sp.wait_ge(t_out, 2 * tt + 2)
                sp.dma_start(a["out"][tt * P:(tt + 1) * P, :], t[:, tt, :]).then_inc(out_st, 16)
            sp.wait_ge(out_st, 16 * TT)

        @block.gpsimd
        def _(pool):
            def split_expert(e):
                b = e % 2
                for n in range(2 * WQ):
                    piece, q = (piece1, n) if n < WQ else (piece2, n - WQ)
                    raw_w, hi, lo = (w1_raw[b], w1_hi[b], w1_lo[b]) if n < WQ else (w2_raw[b], w2_hi[b], w2_lo[b])
                    pool.wait_ge(ld_1[b][n], 16 * (e // 2 + 1))
                    pool.tensor_scalar(piece(hi, q), piece(raw_w, q), 1.0, 1.0, ALU.mult, ALU.mult).then_inc(w_hi, 1)
                    pool.wait_ge(w_hi, 2 * WQ * e + n + 1)
                    pool.tensor_tensor(piece(lo, q), piece(raw_w, q), piece(hi, q).bitcast(F32), ALU.subtract).then_inc(w_ok[b], 1)

            pool.wait_ge(pv_ok[1], TT * NH)
            for i in L2:
                pool.wait_ge(st_o[1][i], 16 * NH)
            split_expert(0)
            pool.wait_ge(where_ok, 1)
            pool.wait_ge(zero_st, 16 * (2 * (TILES + 1) - 2 * TT))
            for r in range(2):
                for tt in range(TT):
                    pool.indirect_dma_start(
                        out=xs_dram[:, :], out_offset=bass.IndirectOffsetOnAxis(ap=where_i[:, r, tt:tt + 1], axis=0),
                        in_=tn[:, tt, :], in_offset=None).then_inc(scattered, 16)
            for e in range(1, NE):
                split_expert(e)
            pool.wait_ge(y_all, 1)
            for tt in range(TT):
                for r in range(2):
                    pool.indirect_dma_start(
                        out=gy[:, r, tt, :], out_offset=None, in_=ys_dram[:, :],
                        in_offset=bass.IndirectOffsetOnAxis(ap=where_i[:, r, tt:tt + 1], axis=0)).then_inc(gathered[tt], 16)

        @block.tensor
        def _(pe):
            mm = pe.matmul
            for r in range(2):
                pe.wait_ge(consts, 4 + r)
                if r == 0:
                    pe.wait_ge(ld_x, 48)
                for m in range(KT):
                    for k in range(KT):
                        g = k * KT + m
                        lhs = grp[:, g, :] if g < 8 else qf[:, 1, 0:P]
                        last = mm(ps[:, r, m:m + 1], lhs, mv[:, k, 0:1] if r == 0 else gd[:, k:k + 1],
                                  start=(k == 0), stop=(k == KT - 1))
                last.then_inc(g_sum, 1)

            for L in L2:
                pe.wait_ge(xn_ok[L], KT if L == 0 else TT)
                pe.wait_ge(ld_w[L], 16)
                for u in range(2 * KT):
                    wait(pe, qk_ev[L], u - 1)
                    for half in range(2):
                        for k in range(KT):
                            last = mm(ps[:, 2 * (u % 2) + half, :], wqkv[:, k, u * P:(u + 1) * P],
                                      xnT[:, k, half * HALF:(half + 1) * HALF], start=(k == 0), stop=(k == KT - 1))
                    last.then_inc(qk_mm[L], 1)
                for tt in range(TT):
                    wait(pe, v_ev[L], tt - 3)
                    for k in range(KT):
                        last = mm(ps[:, 4 + tt % 4, 0:C], xnT[:, k, tt * P:(tt + 1) * P],
                                  wqkv[:, k, 2 * C:3 * C], start=(k == 0), stop=(k == KT - 1))
                    last.then_inc(v_mm[L], 1)
                if L == 0:
                    pe.wait_ge(qk_ev[0], 2 * KT)
                    pe.wait_ge(bd_ok, 4)
                    for w in range(2):
                        for i in range(SIDE // 4):
                            n = 8 * w + i
                            wait(pe, rel_ev, n - 3)
                            for j in range(4):
                                s = 4 * i + j
                                q = qf[:, :, :].rearrange("p g (h w) -> p g h w", w=SIDE)
                                rhs = q[:, :, s, :] if w == 0 else q[:, :, :, s]
                                last = mm(ps[:, n % 4, 96 * j:96 * j + 96], bd[:, w, SIDE - 1 - s:REL - s, :].rearrange("p i a -> p (i a)"),
                                          rhs, start=True, stop=True)
                            last.then_inc(rel_mm, 1)
                    pe.wait_ge(rel_ev, 16)
                pe.wait_ge(v_ev[L], TT)
                pe.wait_ge(qk_ev[L], 2 * KT)
                pe.wait_ge(ld_e, 32)

                n_m, n_a = (4, 11) if L == 0 else (2, 7)
                kr = 96 if L == 0 else 32

                def max_scores(h, b, qt):
                    wait(pe, mx_ok[L], TT * h + qt)
                    if qt == 0:
                        pe.wait_ge(ld_m[L][b], (h - b) * 8 * n_m + 16 * n_m)
                    for half in range(2):
                        last = mm(ps[:, half, :], qm[b][0:kr, qt * P:(qt + 1) * P],
                                  km[b][0:kr, half * HALF:(half + 1) * HALF], start=True, stop=True)
                    last.then_inc(sm_ok[L], 1)

                def turn_max(h, b):
                    pe.wait_ge(mx_ok[L], TT * (h + 1))
                    wait(pe, o_ok[L], h - 1)
                    pe.transpose(ps[0:TT, 6 + b, 0:P], mcol[:, b, :], ident[:]).then_inc(mT_ok[L], 1)

                def scores(h, b, s):
                    if s == 0:
                        pe.wait_ge(ld_a[L][b], (h - b) * 8 * n_a + 16 * n_a)
                        pe.wait_ge(r_ok[L], h + 1)
                    wait(pe, p_ok[L], TT * h + s - 1)
                    for half in range(2):
                        out = ps[:, 2 + 2 * (s % 2) + half, :]
                        cols = slice(half * HALF, (half + 1) * HALF)
                        last = mm(out, ka[b][:, s * P:(s + 1) * P], qa[b][:, cols], start=True, stop=(L == 1))
                        if L == 0:
                            last = mm(out, eb[:, s * P:(s + 1) * P], qb[b][:, cols], start=False, stop=True)
                    last.then_inc(st_ok[L], 1)

                def out_product(h, b, s):
                    pe.wait_ge(p_ok[L], TT * h + s + 1)
                    if s == 0:
                        wait(pe, o_ok[L], h - 1)
                    for c in range(4):
                        half = c % 2
                        last = mm(ps[HD * c:HD * c + HD, 6 + b, :], ones[:, 0:HD] if c < 2 else va[b][:, s, :],
                                  prob[:, s % NP, half * HALF:(half + 1) * HALF], start=(s == 0), stop=(s == TT - 1))
                    last.then_inc(pv_ok[L], 1)

                def head(h, b, first=False, left=2):
                    for s in range(TT):
                        scores(h, b, s)
                        if s < 6 and left >= 1:
                            max_scores(h + 1, 1 - b, s + 2)
                        if s == 7 and left >= 1:
                            turn_max(h + 1, 1 - b)
                        if s >= 6 and left >= 2:
                            max_scores(h + 2, b, s - 6)
                        if s > 0:
                            out_product(h, b, s - 1)
                        elif not first:
                            out_product(h - 1, 1 - b, TT - 1)

                for m in range(TT):
                    max_scores(0, 0, m)
                turn_max(0, 0)
                max_scores(1, 1, 0)
                max_scores(1, 1, 1)
                head(0, 0, first=True)
                head(1, 1)
                with pe.Fori(1, NH // 2 - 1) as i:
                    head(2 * i, 0)
                    head(2 * i + 1, 1)
                head(NH - 2, 0, left=1)
                head(NH - 1, 1, left=0)
                out_product(NH - 1, 1, TT - 1)

                pe.wait_ge(o_ok[L], NH)
                pe.wait_ge(ld_o[L], 16)
                pe.wait_ge(ld_w[L], 32)
                for tt in range(TT):
                    wait(pe, t_ok[L], tt - 3)
                    for k in range(KT):
                        last = mm(ps[:, tt % 4, 0:C], oT[:, k, tt * P:(tt + 1) * P], wproj[:, k, :],
                                  start=(k == 0), stop=(k == KT - 1))
                    last.then_inc(pj_mm[L], 1)
                for tt in range(TT):
                    pe.wait_ge(tn_ok[L], tt + 1)
                    wait(pe, xn_ok[L + 1], tt - 1)
                    for k in range(KT):
                        last = pe.transpose(ps[:, 4 + tt % 2, k * P:(k + 1) * P], tn[:, tt, k * P:(k + 1) * P], ident[:])
                    last.then_inc(tr_mm[L], 1)

            pe.wait_ge(xn_ok[2], TT)
            for tt in range(TT):
                for k in range(KT):
                    last = mm(ps[:, 6, tt * NE:(tt + 1) * NE], xnT[:, k, tt * P:(tt + 1) * P], gate[:, k, :],
                              start=(k == 0), stop=(k == KT - 1))
            last.then_inc(lg_mm, 1)
            pe.wait_ge(sel_ok, 1)
            mm(ps[:, 7, 0:(TT + 1) * NE], before[:], taken[:], start=True, stop=False)
            for tt in range(TT):
                rest = TT - tt
                last = mm(ps[:, 7, (tt + 1) * NE:(TT + 1) * NE], ones[:],
                          taken[:, tt:tt + 1, :].broadcast_to([P, rest, NE]), start=False, stop=(tt == TT - 1))
            last.then_inc(cnt_mm, 1)

            def turn(n):
                pe.wait_ge(x_ld, 16 * n + 16)
                wait(pe, x_lo, n)
                wait(pe, x_hi, n)
                for k in range(KT):
                    last = pe.transpose(ps[:, 7, k * P:(k + 1) * P], xs[:, k * P:(k + 1) * P], ident[:])
                last.then_inc(x_mm, 1)

            pe.wait_ge(cum_ok, 1)
            pe.wait_ge(where_ok, 1)
            turn(0)
            with pe.Fori(0, NE // 2) as pair:
                for b in L2:
                    e = pair * 2 + b
                    begin = pe.value_load(cum_i[0:1, bass.ds(e, 1)], min_val=0, max_val=TILES - 1)
                    end = pe.value_load(cum_i[0:1, bass.ds(e + 1, 1)], min_val=1, max_val=TILES)
                    with pe.Fori(begin, end) as j:
                        pe.wait_ge(x_hi, j + 1)
                        pe.wait_ge(x_lo, j + 1)
                        for g in range(HC // 2):
                            if 2 * g % WC == 0:
                                pe.wait_ge(w_ok[b], pair * (2 * WQ) + 2 * g // WC + 1)
                            pe.wait_ge(h_s_ok, j * (HC // 2) + g + 1)
                            for c in (2 * g, 2 * g + 1):
                                out = ps[:, g, 2 * P * (c % 2):2 * P * (c % 2) + 2 * P]
                                for k in range(KT):
                                    mm(out, w1_hi[b][:, k, c * P:(c + 1) * P], x2[:, k, :, :],
                                       start=(k == 0 and c % 2 == 0), stop=False, skip_group_check=True)
                                    last = mm(out[:, 0:P], w1_lo[b][:, k, c * P:(c + 1) * P], x2[:, k, 0, :],
                                              start=False, stop=(k == KT - 1), skip_group_check=True)
                            last.then_inc(h_mm, 1)
                        turn(j + 1)
                        pe.wait_ge(y_ev, j + 1)
                        for c in range(HC):
                            if c % WC == 0:
                                pe.wait_ge(w_ok[b], pair * (2 * WQ) + WQ + c // WC + 1)
                            if c % 2 == 0:
                                pe.wait_ge(h_l_ok, j * (HC // 2) + c // 2 + 1)
                            for n, (h, w) in enumerate(((h_hi, w2_hi[b]), (h_hi, w2_lo[b]), (h_lo, w2_hi[b]))):
                                last = mm(ps[:, 6, 0:C], h[:, c, :], w[:, c, :],
                                          start=(c == 0 and n == 0), stop=(c == HC - 1 and n == 2))
                        last.then_inc(y_mm, 1)

        @block.vector
        def _(v):
            done = [0]

            def own(ins):
                done[0] += 1
                ins.then_inc(dv, 1)
                v.wait_ge(dv, done[0])

            own(v.memset(bd[:], 0.0))
            for i in L2:
                v.memset(f(ka[i][96:104, :]), 1.0)
            v.memset(zero[:], 0.0)
            v.memset(ones[:], 1.0).then_inc(consts, 2)
            v.sem_inc(y_ev, 1)
            v.sem_inc(y_st, 16)
            v.sem_inc(h_s_ok, HC // 2)
            v.wait_ge(ld_c, 16 * 19)
            v.tensor_copy(eb[:], ebf).then_inc(consts, 1)
            for g in range(4):
                rows = slice(g * HD, (g + 1) * HD)
                v.tensor_copy(bd[rows, :, :, g], tab[rows]).then_inc(bd_ok, 1)
            v.wait_ge(ld_x, 48)
            for k in range(KT):
                for half in range(2):
                    own(v.bn_stats(stat[:, k, 6 * half:6 * half + 6], xnT[:, k, half * HALF:(half + 1) * HALF]))
                last = v.bn_aggr(mv[:, k, :], stat[:, k, :])
                own(last)
            v.sem_inc(consts, 1)
            v.wait_ge(g_sum, 1)
            own(v.tensor_copy(gm[:, :, 0], ps[:, 0, 0:KT]))
            own(v.tensor_tensor(gd[:], mv[:, 0:KT, 0], gm[:, :, 0], ALU.subtract))
            own(v.tensor_tensor(gd[:], gd[:], gd[:], ALU.mult))
            own(v.tensor_tensor(gd[:], gd[:], mv[:, 0:KT, 1], ALU.add))
            v.sem_inc(consts, 1)
            v.wait_ge(g_sum, 2)
            v.tensor_scalar(gm[:, :, 1], ps[:, 1, 0:KT], 1e-5, None, ALU.add).then_inc(lx, 1)
            v.wait_ge(av, 1)
            own(v.reciprocal(rstd[:, 0:KT], sd[:, 0:KT]))
            for k in range(KT):
                v.tensor_scalar(xnT[:, k, :], xnT[:, k, :], gm[:, k, 0:1], rstd[:, k:k + 1],
                                ALU.subtract, ALU.mult).then_inc(xn_ok[0], 1)

            for L in L2:
                n = 0
                for u in range(2 * KT):
                    src = qf[:, u, :] if u < KT else kf[:, u % 2, :]
                    s = SCALE[L] if u < KT else 1.0
                    v.wait_ge(qk_ev[L], u + 1)
                    hi, lo = stage[:, n % 4, :], stage[:, (n + 1) % 4, :]
                    wait(v, st_s[L][n % 4], stored(n))
                    wait(v, st_s[L][(n + 1) % 4], stored(n + 1))
                    ins = v.tensor_scalar(hi, src, s, None, ALU.mult).then_inc(split[L], 1)
                    v.wait_ge(split[L], n + 1)
                    v.scalar_tensor_tensor(lo, src, s, f(hi), ALU.mult, ALU.subtract).then_inc(split[L], 1)
                    n += 2
                for tt in range(TT):
                    v.wait_ge(v_mm[L], tt + 1)
                    if L == 0:
                        v.tensor_tensor(vf[:, tt, :], ps[:, 4 + tt % 4, 0:C], bv[:], ALU.add).then_inc(v_ev[L], 1)
                    else:
                        v.tensor_copy(vf[:, tt, :], ps[:, 4 + tt % 4, 0:C]).then_inc(v_ev[L], 1)
                if L == 0:
                    rel = prob[:, 0:KT, :]
                    for w in range(2):
                        view = rel.rearrange("p g (h w) -> p g h w", w=SIDE)
                        for i in range(SIDE // 4):
                            v.wait_ge(rel_mm, 8 * w + i + 1)
                            if w == 1 and i == 0:
                                v.wait_ge(split[L], n)
                            for g in range(KT):
                                src = ps[:, (8 * w + i) % 4, 0:C].rearrange("p (j g x) -> p g j x", j=4, g=KT)[:, g]
                                dst = view[:, g, 4 * i:4 * i + 4, :] if w == 0 else \
                                    view[:, g, :, 4 * i:4 * i + 4].rearrange("p h j -> p j h")
                                ins = v.tensor_copy(dst, src)
                            ins.then_inc(rel_ev, 1)
                        v.wait_ge(rel_ev, 8 * w + 8)
                        for g in range(KT):
                            hi, lo = stage[:, n % 4, :], stage[:, (n + 1) % 4, :]
                            wait(v, st_s[L][n % 4], stored(n))
                            wait(v, st_s[L][(n + 1) % 4], stored(n + 1))
                            v.tensor_copy(hi, rel[:, g, :]).then_inc(split[L], 1)
                            v.wait_ge(split[L], n + 1)
                            v.tensor_tensor(lo, rel[:, g, :], f(hi), ALU.subtract).then_inc(split[L], 1)
                            n += 2
                v.wait_ge(split[L], n)

                def maximum(h, b, qt):
                    v.wait_ge(sm_ok[L], TT * h + qt + 1)
                    if qt == 0:
                        wait(v, mT_ok[L], h - 1)
                    v.tensor_reduce(mcol[:, b, qt:qt + 1], ps[:, 0:2, :], AX.XY, ALU.max).then_inc(mx_ok[L], 1)

                def place_max(h, b):
                    v.wait_ge(mT_ok[L], h + 1)
                    wait(v, st_ok[L], TT * (h - 1))
                    v.tensor_tensor(qa[b][96:104, :].rearrange("p (t q) -> p t q", q=P),
                                    ps[0:TT, 6 + b, 0:P].unsqueeze(1).broadcast_to([TT, TT, P]),
                                    negd[:], ALU.mult).then_inc(r_ok[L], 1)

                def invert_sums(h, b, part):
                    cols = slice(part * P, (part + 1) * P)
                    v.wait_ge(pv_ok[L], TT * (h + 1))
                    wait(v, o_ok[L], h)
                    v.reciprocal(rec[:, cols], ps[0:2 * HD, 6 + b, cols]).then_inc(o_rc[L], 1)

                def output(h, b):
                    wait(v, st_o[L][b], 16 * (h - b))
                    v.wait_ge(o_rc[L], 4 * (h + 1))
                    v.tensor_tensor(osb[b], ps[2 * HD:P, 6 + b, :], rec, ALU.mult).then_inc(o_ok[L], 1)

                def head(h, b, first=False, left=2):
                    for s in range(TT):
                        if s < 6 and left >= 1:
                            maximum(h + 1, 1 - b, s + 2)
                        if s == 7 and left >= 1:
                            place_max(h + 1, 1 - b)
                        if s >= 6 and left >= 2:
                            maximum(h + 2, b, s - 6)
                        if 1 <= s <= 4 and not first:
                            invert_sums(h - 1, 1 - b, s - 1)
                        if s == 5 and not first:
                            output(h - 1, 1 - b)

                for m in range(TT):
                    maximum(0, 0, m)
                place_max(0, 0)
                maximum(1, 1, 0)
                maximum(1, 1, 1)
                head(0, 0, first=True)
                head(1, 1)
                with v.Fori(1, NH // 2 - 1) as i:
                    head(2 * i, 0)
                    head(2 * i + 1, 1)
                head(NH - 2, 0, left=1)
                head(NH - 1, 1, left=0)
                for part in range(4):
                    invert_sums(NH - 1, 1, part)
                output(NH - 1, 1)

                own(v.tensor_tensor(t[:], t[:], bproj[:, L:L + 1, :].broadcast_to([P, TT, C]), ALU.add))
                for tt in range(TT):
                    v.wait_ge(pj_mm[L], tt + 1)
                    v.tensor_tensor(t[:, tt, :], t[:, tt, :], ps[:, tt % 4, 0:C], ALU.add).then_inc(t_ok[L], 1)
                    v.wait_ge(t_ok[L], tt + 1)
                    own(v.bn_stats(stat[:, tt, 0:6], t[:, tt, :]))
                    own(v.bn_aggr(mv[:, tt, :], stat[:, tt, 0:6]))
                v.tensor_scalar(m8[:], mv[:, :, 1], 1e-5, None, ALU.add).then_inc(lx, 1)
                v.wait_ge(av, 2 + L)
                own(v.reciprocal(rstd[:], sd[:]))
                for tt in range(TT):
                    v.tensor_scalar(tn[:, tt, :], t[:, tt, :], mv[:, tt, 0:1], rstd[:, tt:tt + 1],
                                    ALU.subtract, ALU.mult).then_inc(tn_ok[L], 1)

            v.wait_ge(lg_mm, 1)
            own(v.tensor_tensor(lg[:], ps[:, 6, 0:TT * NE].rearrange("p (t e) -> p t e", e=NE),
                                gateb[:].unsqueeze(1).broadcast_to([P, TT, NE]), ALU.add))
            v.sem_inc(lg_ev, 1)
            own(v.tensor_reduce(m8[:], lg[:], AX.X, ALU.max))
            v.tensor_tensor(lg[:], lg[:], m8[:].unsqueeze(2).broadcast_to([P, TT, NE]), ALU.subtract).then_inc(lx, 1)
            v.wait_ge(av, 4)
            own(v.tensor_reduce(s8[:], pr[:], AX.X, ALU.add))
            own(v.reciprocal(s8[:], s8[:]))
            own(v.tensor_tensor(pr[:], pr[:], s8[:].unsqueeze(2).broadcast_to([P, TT, NE]), ALU.mult))
            mine = pr[:].unsqueeze(3).broadcast_to([P, TT, NE, NE])
            other = pr[:].unsqueeze(2).broadcast_to([P, TT, NE, NE])
            own(v.tensor_tensor(cm[:], other, mine, ALU.is_gt))
            own(v.tensor_tensor(cm2[:], other, mine, ALU.is_equal))
            v.wait_ge(ld_g, 32)
            own(v.tensor_tensor(cm2[:], cm2[:], first[:].unsqueeze(1).broadcast_to([P, TT, NE, NE]), ALU.mult))
            own(v.tensor_tensor(cm[:], cm[:], cm2[:], ALU.add))
            own(v.tensor_reduce(rk[:], cm[:], AX.X, ALU.add))
            own(v.memset(taken[:], 0.0))
            own(v.tensor_scalar(taken[:, 0:TT, :], rk[:], 1.5, None, ALU.is_lt))
            v.sem_inc(sel_ok, 1)
            own(v.tensor_scalar(choice[:, 0], rk[:], 0.5, None, ALU.is_lt))
            own(v.tensor_tensor(choice[:, 1], taken[:, 0:TT, :], choice[:, 0], ALU.subtract))
            own(v.tensor_tensor(w8[:], taken[:, 0:TT, :], pr[:], ALU.mult))
            own(v.tensor_reduce(s8[:], w8[:], AX.X, ALU.add))
            own(v.reciprocal(s8[:], s8[:]))
            own(v.tensor_tensor(w8[:], w8[:], s8[:].unsqueeze(2).broadcast_to([P, TT, NE]), ALU.mult))
            own(v.tensor_tensor(prod[:], choice[:], w8[:].unsqueeze(1).broadcast_to([P, 2, TT, NE]), ALU.mult))
            own(v.tensor_reduce(wts[:], prod[:], AX.X, ALU.add))
            v.wait_ge(cnt_mm, 1)
            places = ps[:, 7, 0:TT * NE].rearrange("p (t e) -> p t e", e=NE)
            count = ps[:, 7, TT * NE:(TT + 1) * NE]
            own(v.tensor_tensor(cm[:, 0], count.unsqueeze(2).broadcast_to([P, NE, NE]), above[:], ALU.is_gt))
            own(v.tensor_reduce(ntile[:], cm[:, 0], AX.X, ALU.add))
            own(v.tensor_tensor(cm[:, 1], first[:], ntile[:].unsqueeze(1).broadcast_to([P, NE, NE]), ALU.mult))
            own(v.tensor_reduce(cum[:, 0:NE], cm[:, 1], AX.X, ALU.add))
            own(v.tensor_tensor(cum[:, NE:NE + 1], cum[:, NE - 1:NE], ntile[:, NE - 1:NE], ALU.add))
            own(v.tensor_copy(cum_i[:], cum[:]))
            v.sem_inc(cum_ok, 1)
            own(v.tensor_scalar(cum[:], cum[:], float(P), None, ALU.mult))
            own(v.tensor_tensor(slot[:], places, cum[:, 0:NE].unsqueeze(1).broadcast_to([P, TT, NE]), ALU.add))
            own(v.tensor_tensor(prod[:], choice[:], slot[:].unsqueeze(1).broadcast_to([P, 2, TT, NE]), ALU.mult))
            own(v.tensor_reduce(where[:], prod[:], AX.X, ALU.add))
            own(v.tensor_copy(where_i[:], where[:]))
            v.sem_inc(where_ok, 1)

            def turned(n):
                v.wait_ge(x_hi, n + 1)
                v.tensor_tensor(x2[:, :, 1, :], ps[:, 7, 0:C].rearrange("p (k q) -> p k q", k=KT),
                                f(x2[:, :, 0, :]), ALU.subtract).then_inc(x_lo, 1)

            turned(0)
            with v.Fori(0, NE // 2) as pair:
                for b in L2:
                    e = pair * 2 + b
                    begin = v.value_load(cum_i[0:1, bass.ds(e, 1)], min_val=0, max_val=TILES - 1)
                    end = v.value_load(cum_i[0:1, bass.ds(e + 1, 1)], min_val=1, max_val=TILES)
                    with v.Fori(begin, end) as j:
                        def bank(g):
                            return j * (HC // 2) + g

                        for g in range(HC // 2):
                            v.wait_ge(h_b_ok, bank(g) + 1)
                            part = ps[:, g, :].rearrange("p (c a q) -> p c a q", c=2, a=2)[:, :, 0, :]
                            v.tensor_tensor(h_sum[:, g % 2], part, h_b[:, g % 2], ALU.add).then_inc(h_s_ok, 1)
                            v.wait_ge(h_s_ok, bank(g) + 1 + HC // 2)
                            hi = h_hi[:, 2 * g:2 * g + 2, :]
                            v.tensor_scalar(hi, h_sum[:, g % 2], 0.0, None, ALU.max).then_inc(h_h_ok, 1)
                            v.wait_ge(h_h_ok, bank(g) + 1)
                            v.scalar_tensor_tensor(h_lo[:, 2 * g:2 * g + 2, :].rearrange("p c q -> p (c q)"),
                                                   h_sum[:, g % 2].rearrange("p c q -> p (c q)"), 0.0,
                                                   f(hi).rearrange("p c q -> p (c q)"),
                                                   ALU.max, ALU.subtract).then_inc(h_l_ok, 1)
                        turned(j + 1)
                        v.wait_ge(y_mm, j + 1)
                        v.wait_ge(ld_b[b], pair * 32 + 32)
                        v.wait_ge(y_st, j * 16 + 16)
                        v.tensor_tensor(ysb[:], ps[:, 6, 0:C], b2c[b][:], ALU.add).then_inc(y_ev, 1)

            for tt in range(TT):
                v.wait_ge(gathered[tt], 32)
                for r in range(2):
                    v.scalar_tensor_tensor(t[:, tt, :], gy[:, r, tt, :], wts[:, r, tt:tt + 1], t[:, tt, :],
                                           ALU.mult, ALU.add).then_inc(t_out, 1)
                    v.wait_ge(t_out, 2 * tt + r + 1)

        @block.scalar
        def _(act):
            act.wait_ge(lx, 1)
            act.activation(sd[:, 0:KT], gm[:, :, 1], ACT.Sqrt).then_inc(av, 1)
            for L in L2:
                for u in range(2 * KT):
                    act.wait_ge(qk_mm[L], u + 1)
                    if u >= KT + 2:
                        act.wait_ge(split[L], 2 * (u - 1))
                    dst = qf[:, u, :] if u < KT else kf[:, u % 2, :]
                    src = ps[:, 2 * (u % 2):2 * (u % 2) + 2, :].rearrange("p a b -> p (a b)")
                    if L == 0:
                        act.activation(dst, src, ACT.Identity, bias=bqk[:, u:u + 1]).then_inc(qk_ev[L], 1)
                    else:
                        act.activation(dst, src, ACT.Copy).then_inc(qk_ev[L], 1)
                if L == 0:
                    act.wait_ge(split[0], 24)

                def head(h, b, first=False):
                    for s in range(TT):
                        act.wait_ge(st_ok[L], TT * h + s + 1)
                        wait(act, pv_ok[L], TT * h + s + 1 - NP)
                        act.activation(prob[:, s % NP, :], ps[:, 2 + 2 * (s % 2):4 + 2 * (s % 2), :].rearrange("p a b -> p (a b)"),
                                       ACT.Exp).then_inc(p_ok[L], 1)
                        if s == 6 and not first:
                            store(h - 1, 1 - b)

                def store(h, b):
                    rows = hrow(act, h)
                    act.wait_ge(o_ok[L], h + 1)
                    for half in range(2):
                        act.dma_start(att_dram[L][rows, half * HALF:(half + 1) * HALF],
                                      osb[b][half * HD:(half + 1) * HD, :]).then_inc(st_o[L][b], 16)

                head(0, 0, first=True)
                head(1, 1)
                with act.Fori(1, NH // 2 - 1) as i:
                    head(2 * i, 0)
                    head(2 * i + 1, 1)
                head(NH - 2, 0)
                head(NH - 1, 1)
                store(NH - 1, 1)
                act.wait_ge(lx, 2 + L)
                act.activation(sd[:], m8[:], ACT.Sqrt).then_inc(av, 1)
                for tt in range(TT):
                    act.wait_ge(tr_mm[L], tt + 1)
                    act.activation(xnT[:, :, tt * P:(tt + 1) * P],
                                   ps[:, 4 + tt % 2, 0:C].rearrange("p (k q) -> p k q", k=KT), ACT.Copy).then_inc(xn_ok[L + 1], 1)
            act.wait_ge(lx, 4)
            act.activation(pr[:], lg[:], ACT.Exp).then_inc(av, 1)

            def turned(n):
                act.wait_ge(x_mm, n + 1)
                act.activation(x2[:, :, 0, :], ps[:, 7, 0:C].rearrange("p (k q) -> p k q", k=KT), ACT.Copy).then_inc(x_hi, 1)

            turned(0)
            act.wait_ge(cum_ok, 1)
            with act.Fori(0, NE // 2) as pair:
                for b in L2:
                    e = pair * 2 + b
                    begin = act.value_load(cum_i[0:1, bass.ds(e, 1)], min_val=0, max_val=TILES - 1)
                    end = act.value_load(cum_i[0:1, bass.ds(e + 1, 1)], min_val=1, max_val=TILES)
                    with act.Fori(begin, end) as j:
                        act.wait_ge(ld_b[b], pair * 32 + 32)
                        for g in range(HC // 2):
                            act.wait_ge(h_mm, j * (HC // 2) + g + 1)
                            act.wait_ge(h_s_ok, j * (HC // 2) + g + HC // 2 - 1)
                            for c in L2:
                                last = act.activation(h_b[:, g % 2, c, :], ps[:, g, 2 * P * c + P:2 * P * c + 2 * P],
                                                      ACT.Identity, bias=b1c[b][:, 2 * g + c:2 * g + c + 1])
                            last.then_inc(h_b_ok, 1)
                        turned(j + 1)


def constants():
    key = np.arange(N)
    rows = np.arange(SIDE)[:, None]
    pos = np.concatenate([key // SIDE == rows, key % SIDE == rows])
    group = np.arange(C) // GROUP
    same = (group[:, None] == group[None, :]) / np.float32(GROUP)
    blocks = same.reshape(KT, P, KT, P).transpose(0, 2, 1, 3).reshape(KT * KT, P, P)
    negd = np.zeros((TT, TT, P), np.float32)
    for i in range(TT):
        negd[i, i] = -1.0
    low = np.broadcast_to(np.tril(np.ones((NE, NE)), -1), (P, NE, NE))
    above = np.broadcast_to(np.array([-1] + [i * P for i in range(1, NE)]), (P, NE, NE))
    return {
        "ident": np.eye(P, dtype=np.float32), "grp": blocks.astype(np.float32),
        "eb": np.concatenate([pos, pos]).astype(np.float32), "negd": negd,
        "low": np.ascontiguousarray(low, np.float32), "above": np.ascontiguousarray(above, np.float32),
        "before": np.triu(np.ones((P, P), np.float32), 1),
    }


def kernel(x, L0_conv_qkv_w, L0_conv_qkv_b, L0_conv_proj_w, L0_conv_proj_b, L0_conv_rel_pos_h, L0_conv_rel_pos_w,
           L1_attn_w_qkv, L1_attn_w_proj, L1_attn_b_proj, L1_ffn_gate_w, L1_ffn_gate_b, L1_ffn_w1, L1_ffn_b1,
           L1_ffn_w2, L1_ffn_b2):
    import concourse.bacc as bacc
    from concourse.bass_utils import run_bass_kernel_spmd as run

    tokens = np.asarray(x).reshape(N, C)
    arrays = {
        "x": tokens, "xT": tokens.T,
        "wqkv0": np.asarray(L0_conv_qkv_w).T, "wqkv1": np.asarray(L1_attn_w_qkv).T,
        "bqk": np.asarray(L0_conv_qkv_b)[:2 * C].reshape(2 * KT, P).T, "bv": np.asarray(L0_conv_qkv_b)[2 * C:],
        "wproj0": np.asarray(L0_conv_proj_w).T, "bproj0": np.asarray(L0_conv_proj_b),
        "wproj1": np.asarray(L1_attn_w_proj).T, "bproj1": np.asarray(L1_attn_b_proj),
        "relh": np.asarray(L0_conv_rel_pos_h)[::-1].T, "relw": np.asarray(L0_conv_rel_pos_w)[::-1].T,
        "gate": np.asarray(L1_ffn_gate_w).T, "gateb": np.asarray(L1_ffn_gate_b),
        "w1": np.asarray(L1_ffn_w1).transpose(0, 2, 1), "b1": np.asarray(L1_ffn_b1).reshape(NE, HC, P).transpose(0, 2, 1),
        "w2": np.asarray(L1_ffn_w2).transpose(0, 2, 1), "b2": np.asarray(L1_ffn_b2),
    }
    arrays.update(constants())
    arrays = {k: np.ascontiguousarray(v) for k, v in arrays.items()}
    nc = bacc.Bacc("TRN2", target_bir_lowering=False, num_devices=1)
    aps = {k: nc.dram_tensor(f"in_{k}", v.shape, mybir.dt.from_np(v.dtype), kind="ExternalInput").ap()
           for k, v in arrays.items()}
    aps["out"] = nc.dram_tensor("out_0", (N, C), F32, kind="ExternalOutput").ap()
    build_program(nc, aps)
    result = run(nc, [{f"in_{k}": v for k, v in arrays.items()}], core_ids=[0])
    return np.asarray(result.results[0]["out_0"]).reshape(np.shape(x))
```

```python
from contextlib import ExitStack

import numpy as np
import concourse.bass as bass
from concourse import mybir

F32 = mybir.dt.float32
F32R = mybir.dt.float32r
I32 = mybir.dt.int32
U32 = mybir.dt.uint32
ALU = mybir.AluOpType
ACT = mybir.ActivationFunctionType
AX = mybir.AxisListType

P = 128
C = 384
KT = C // P
SIDE = 32
N = SIDE * SIDE
TT = N // P
NH = 12
HD = C // NH
HALF = 512
QUARTER = N // 4
EARLY = (2, 0)
BETWEEN = (([], [], [], [], [], [], [(0, 0), (0, 1)], [(0, 2), (0, 3), (0, 4), (0, 5), (0, 6), (0, 7), (1, 0), (1, 1), (1, 2), (1, 3), (1, 4)]),
           ([(0, 0), (0, 1)], [(0, 2)], [(0, 3), (0, 4)], [(0, 5)], [(0, 6), (0, 7)], [(1, 0)], [(1, 1), (1, 2)], [(1, 3), (1, 4)]))
TURN = (7, 5)
AHEAD = 5
PLACED = (0, 2, 4, 6, 8)
MAXIMA = [[(1, s + AHEAD)] if s < TT - AHEAD else [(2, s - TT + AHEAD)] for s in range(TT)]
MAXIMA_FIRST = [[(1, 5)], [(1, 6)], [(1, 7)], [(2, 0)], [(2, 1)], [(2, 2)], [(2, 3)], [(2, 4)]]
BEHIND = 2
ADDS = (5, 4)
NE = 8
HID = 4 * C
HC = HID // P
GROUP = C // 32
HG = HALF // P
HGS = HC // HG
REL = 2 * SIDE - 1
SCALE = (HD ** -0.5, C ** -0.5)
NP = 5
WQ = 3
WN = HID // WQ
WC = HC // WQ
TILES = 2 * TT + NE - 1
FILLED = 32

SLOTS = (("Q_LO", "Q_HI", "RH_HI", "RW_HI", "RH_LO", "RW_LO", "K_HI", "K_LO"), ("Q_LO", "Q_HI", "K_HI", "K_LO"))
ZERO = 4


def build_program(nc, a):
    ctx = ExitStack()
    with ctx:
        def sem(name):
            return ctx.enter_context(nc.semaphore(name))

        def sb(name, shape, dt=F32, where=ctx):
            return where.enter_context(nc.sbuf_tensor(name, shape, dt))

        ps = ctx.enter_context(nc.psum_tensor("ps", [P, 8, HALF], F32))

        heads_dram = [nc.dram_tensor(f"heads{L}", [NH, len(SLOTS[L]), HD, N], F32).ap() for L in range(2)]

        xs_dram = nc.dram_tensor("xs", [FILLED * P, C], F32).ap()
        ys_dram = nc.dram_tensor("ys", [FILLED * P, C], F32).ap()

        t = sb("t", [P, TT, C])
        xnT = sb("xnT", [P, KT, N])
        ident = sb("ident", [P, P])
        before = sb("before", [P, P])
        ones = sb("ones", [P, P])
        bqk = sb("bqk", [P, 6])
        bv = sb("bv", [P, C])
        bproj = sb("bproj", [P, 2, C])
        gate = sb("gate", [P, KT, NE])
        gateb = sb("gateb", [P, NE])
        stat = sb("stat", [P, TT, 12])
        mv = sb("mv", [P, TT, 2])
        sd = sb("sd", [P, TT])
        rstd = sb("rstd", [P, TT])
        gm = sb("gm", [P, KT, 2])
        gd = sb("gd", [P, KT])
        eps = sb("eps", [P, 1])
        spare = sb("spare", [P, 1])
        zero = sb("zero", [P, C])

        def placed(start):
            at = [start]

            def put(name, shape, dt=F32):
                tensor = nc.alloc_sbuf_tensor_at(name, shape, dt, offset=at[0])
                at[0] += -(-int(np.prod(shape[1:])) * 4 // 32) * 32
                return tensor
            return put, at

        first_start = -(-nc.sbuf_base // 32) * 32
        put, first_end = placed(first_start)
        w2_raw0, w1_0 = put("w2_raw0", [P, HC, C]), put("w1_0", [P, KT, HID])
        low0, _ = placed(first_start)
        start = first_end[0]
        put, att_end = placed(start)
        put("parts_end", [P, 12 * N - (HC * C + KT * HID)], F32R)
        parts = nc.alloc_sbuf_tensor_at("parts", [P, KT, 4, N], F32R, offset=first_start)
        vf = put("vf", [P, TT, C])
        wproj = put("wproj", [P, KT, C])
        wqkv = put("wqkv", [P, KT, 3 * C])
        eb = put("eb", [P, N], F32R)
        qa = [put(f"qa{i}", [104, N], F32R) for i in range(2)]
        ka = [put(f"ka{i}", [104, N], F32R) for i in range(2)]
        qm = [put(f"qm{i}", [96, N], F32R) for i in range(2)]
        km = [put(f"km{i}", [96, N], F32R) for i in range(2)]
        qb = [put(f"qb{i}", [P, N], F32R) for i in range(2)]
        va = [put(f"va{i}", [P, TT, HD]) for i in range(2)]
        prob = put("prob", [P, NP, N])
        qf = put("qf", [P, KT, N])
        osb = [put(f"osb{i}", [P, QUARTER]) for i in range(2)]
        vsb = put("vsb", [P, 2, QUARTER])
        rec = put("rec", [P, QUARTER])
        bd = put("bd", [P, 2, REL, 4])
        tab = put("tab", [P, 2, REL])
        mhalf = put("mhalf", [P, 2, TT, 2])
        mcol = put("mcol", [P, 2, TT])
        negd = put("negd", [TT, TT])
        kf = prob[:, 0:2, :]
        ebf = prob[:, 3, :]
        grp = qf[:].rearrange("p a b -> p (a b)")[:, 0:KT * KT * P].rearrange("p (g c) -> p g c", c=P)
        acc = [qf[:, i, :] for i in range(2)]
        oT = xnT
        raw, raw_end = placed(start)
        low1, _ = placed(start)
        w2_raw = [w2_raw0, raw("w2_raw1", [P, HC, C])]
        w2_lo = [low0("w2_lo0", [P, HC, C], F32R), low1("w2_lo1", [P, HC, C], F32R)]
        w1 = [w1_0, raw("w1_1", [P, KT, HID])]
        put, moe_end = placed(raw_end[0])
        w2_hi = [None, put("w2_hi1", [P, HC, C], F32R)]
        gather_put, _ = placed(moe_end[0])
        w2_hi[0] = put("w2_hi0", [P, HC, C], F32R)
        h_f = put("h_f", [P, HC, P])
        gy = gather_put("gy", [P, 2, TT, C])
        tn_put, _ = placed(moe_end[0])
        h_hi = put("h_hi", [P, HC, P], F32R)
        h_lo = put("h_lo", [P, HC, P], F32R)
        tn = tn_put("tn", [P, TT, C])
        gate_put, _ = placed(moe_end[0])
        cm = gate_put("cm", [P, TT, NE, NE])
        cm2 = gate_put("cm2", [P, TT, NE, NE])
        xs = put("xs", [P, C])
        xT = put("xT", [P, KT, P])
        ysb = put("ysb", [P, C])
        b1c = [put(f"b1c{i}", [P, HC]) for i in range(2)]
        b2c = [put(f"b2c{i}", [P, C]) for i in range(2)]
        lg = put("lg", [P, TT, NE])
        pr = put("pr", [P, TT, NE])
        w8 = put("w8", [P, TT, NE])
        rk = put("rk", [P, TT, NE])
        first = put("first", [P, NE, NE])
        above = put("above", [P, NE, NE])
        m8 = put("m8", [P, TT])
        s8 = put("s8", [P, TT])
        taken = put("taken", [P, TT + 1, NE])
        choice = put("choice", [P, 2, TT, NE])
        prod = put("prod", [P, 2, TT, NE])
        ntile = put("ntile", [P, NE])
        cum = put("cum", [P, NE + 1])
        cum_i = put("cum_i", [P, NE + 1], I32)
        slot = put("slot", [P, TT, NE])
        where = put("where", [P, 2, TT])
        where_i = put("where_i", [P, 2, TT], U32)
        wts = put("wts", [P, 2, TT])
        assert max(att_end[0], moe_end[0]) <= nc.sbuf_top, (att_end, moe_end)

        ld_x = [sem(f"ld_x{k}") for k in range(KT)]
        ld_grp = sem("ld_grp")
        ld_bq = sem("ld_bq")
        ld_c = sem("ld_c")
        ld_t = sem("ld_t")
        ld_w = [sem(f"ld_w{L}") for L in range(2)]
        ld_v = [sem(f"ld_v{L}") for L in range(2)]
        ld_p = [sem(f"ld_p{L}") for L in range(2)]
        ld_e = sem("ld_e")
        made = sem("made")
        eb_ok = sem("eb_ok")
        gn_ok = sem("gn_ok")
        bd_ok = sem("bd_ok")
        m_free = sem("m_free")
        a_free = sem("a_free")
        dv = sem("dv")
        av = sem("av")
        g_sum = sem("g_sum")
        xn_ok = [sem(f"xn_ok{L}") for L in range(3)]
        L2 = range(2)
        qk_mm = [sem(f"qk_mm{L}") for L in L2]
        qk_ev = [sem(f"qk_ev{L}") for L in L2]
        v_mm = [sem(f"v_mm{L}") for L in L2]
        v_ev = [sem(f"v_ev{L}") for L in L2]
        split = [sem(f"split{L}") for L in L2]
        st_q = [[sem(f"st_q{L}{i}") for i in L2] for L in L2]
        st_r = [sem(f"st_r{i}") for i in L2]
        va_ok = [sem(f"va_ok{L}") for L in L2]
        rel_mm = sem("rel_mm")
        rel_hi = sem("rel_hi")
        rel_ev = sem("rel_ev")
        ld_m = [[sem(f"ld_m{L}{i}") for i in L2] for L in L2]
        ld_a = [[sem(f"ld_a{L}{i}") for i in L2] for L in L2]
        sm_ok = [sem(f"sm_ok{L}") for L in L2]
        mx_ok = [sem(f"mx_ok{L}") for L in L2]
        mc_ok = [sem(f"mc_ok{L}") for L in L2]
        mT_ok = [sem(f"mT_ok{L}") for L in L2]
        r_ok = [sem(f"r_ok{L}") for L in L2]
        st_ok = [sem(f"st_ok{L}") for L in L2]
        p_ok = [sem(f"p_ok{L}") for L in L2]
        pv_ok = [sem(f"pv_ok{L}") for L in L2]
        p_in = sem("p_in")
        a_ok = [sem(f"a_ok{L}") for L in L2]
        s_ok = [sem(f"s_ok{L}") for L in L2]
        vs_ok = [sem(f"vs_ok{L}") for L in L2]
        o_rc = [sem(f"o_rc{L}") for L in L2]
        o_ok = [sem(f"o_ok{L}") for L in L2]
        st_o = [[sem(f"st_o{L}{i}") for i in L2] for L in L2]
        pj_mm = [sem(f"pj_mm{L}") for L in L2]
        tb_ok = sem("tb_ok")
        var_ok = [sem(f"var_ok{L}") for L in L2]
        sq_ok = [sem(f"sq_ok{L}") for L in L2]
        t_ok = [sem(f"t_ok{L}") for L in L2]
        tn_ok = [sem(f"tn_ok{L}") for L in L2]
        tr_mm = [sem(f"tr_mm{L}") for L in L2]
        lg_mm = sem("lg_mm")
        lx = sem("lx")
        ld_g = sem("ld_g")
        w8_ok = sem("w8_ok")
        zero_st = sem("zero_st")
        sel_ok = sem("sel_ok")
        cnt_mm = sem("cnt_mm")
        cum_ok = sem("cum_ok")
        where_ok = sem("where_ok")
        scattered = sem("scattered")
        ld_1 = [[sem(f"ld_1{i}_{q}") for q in range(2 * WQ)] for i in L2]
        ld_b = [sem(f"ld_b{i}") for i in L2]
        w2_hi_ok = [sem(f"w2_hi{i}") for i in L2]
        w2_ok = [sem(f"w2_ok{i}") for i in L2]
        x_ld = sem("x_ld")
        x_mm = sem("x_mm")
        x_ok = sem("x_ok")
        h_mm = sem("h_mm")
        h_f_ok = sem("h_f_ok")
        h_h_ok = sem("h_h_ok")
        h_l_ok = sem("h_l_ok")
        y_mm = sem("y_mm")
        y_ev = sem("y_ev")
        y_st = sem("y_st")
        y_all = sem("y_all")
        gathered = [sem(f"gathered{i}") for i in range(TT)]
        t_out = sem("t_out")
        out_st = sem("out_st")

        def wait(eng, s, value):
            if not isinstance(value, int) or value > 0:
                eng.wait_ge(s, value)

        def f(ap):
            return ap.bitcast(F32)

        def rel_bank(w, i):
            order = "p (j m x) -> p m j x" if w == 0 else "p (j m x) -> p m x j"
            return ps[:, (8 * w + i) % 4, 0:C].rearrange(order, j=4, m=KT)

        def rel_tile(view, w, i):
            return view[:, :, 4 * i:4 * i + 4, :] if w == 0 else view[:, :, :, 4 * i:4 * i + 4]

        def piece1(w, q):
            return w[:, :, q * WN:(q + 1) * WN]

        def piece2(w, q):
            return w[:, q * WC:(q + 1) * WC, :]

        def store_quarter(eng, L, b, g, tile, r):
            eng.dma_start(oT[g * HD:(g + 1) * HD, bass.ds(tile, 1), r * QUARTER:(r + 1) * QUARTER].rearrange("p k n -> p (k n)"),
                          osb[b][r * HD:(r + 1) * HD, :]).then_inc(st_o[L][b], 16)

        def load_expert(eng, e, b):
            first, second = (a[w][bass.ds(e, 1)].rearrange("e (k p) n -> p (e k) n", p=P) for w in ("w1", "w2"))
            for q in range(WQ):
                eng.dma_start(piece1(w1[b], q), piece1(first, q)).then_inc(ld_1[b][q], 16)
            for q in range(WQ):
                eng.dma_start(piece2(w2_raw[b], q), piece2(second, q)).then_inc(ld_1[b][WQ + q], 16)

        def load_biases(eng, e, b):
            eng.dma_start(b1c[b][:], a["b1"][bass.ds(e, 1)].rearrange("e p c -> p (e c)")).then_inc(ld_b[b], 16)
            eng.dma_start(b2c[b][:], a["b2"][bass.ds(e, 1)].rearrange("e c -> (e c)").partition_broadcast(P)).then_inc(ld_b[b], 16)

        block = ctx.enter_context(nc.Block())

        @block.sync
        def _(sp):
            x_T = a["xT"].rearrange("(k p) n -> p k n", p=P)
            for k in range(KT):
                sp.dma_start(xnT[:, k, :], x_T[:, k, :]).then_inc(ld_x[k], 16)
            sp.dma_start(grp, a["grp"].rearrange("g p c -> p g c")).then_inc(ld_grp, 16)

            def load_wqkv(L):
                w = a[f"wqkv{L}"].rearrange("(k p) n -> p k n", p=P)
                sp.dma_start(wqkv[:, :, 0:2 * C], w[:, :, 0:2 * C]).then_inc(ld_w[L], 16)
                sp.dma_start(wqkv[:, :, 2 * C:3 * C], w[:, :, 2 * C:3 * C]).then_inc(ld_v[L], 16)

            load_wqkv(0)
            sp.dma_start(bqk[:], a["bqk"]).then_inc(ld_bq, 16)
            for dst, name in ((ebf, "eb"), (ident[:], "ident"), (negd[:], "negd"), (before[:], "before")):
                sp.dma_start(dst, a[name]).then_inc(ld_c, 16)
            for i, name in enumerate(("relh", "relw")):
                for g in range(4):
                    sp.dma_start(tab[g * HD:(g + 1) * HD, i, :], a[name]).then_inc(ld_c, 16)
            for dst, name in ((bv[:], "bv"), (bproj[:, 0, :], "bproj0"), (bproj[:, 1, :], "bproj1"),
                              (gateb[:], "gateb")):
                sp.dma_start(dst, a[name].partition_broadcast(P)).then_inc(ld_c, 16)
            sp.dma_start(gate[:], a["gate"].rearrange("(k p) e -> p k e", p=P)).then_inc(ld_c, 16)
            sp.dma_start(t[:], a["x"].rearrange("(t p) c -> p t c", p=P)).then_inc(ld_t, 16)
            sp.wait_ge(eb_ok, 1)
            for i in L2:
                sp.dma_start(f(km[i][32:96, :]), f(eb[0:64, :])).then_inc(ld_e, 16)

            for L in L2:
                D = heads_dram[L]
                slot = {name: i for i, name in enumerate(SLOTS[L])}

                def store_qk(m):
                    sp.wait_ge(split[L], 4 * m + 4)
                    for g in range(4):
                        for at, name in ((0, "Q_LO"), (2, "K_HI")):
                            sp.dma_start(D[4 * m + g, slot[name]:slot[name] + 2].rearrange("s d n -> d s n"),
                                         f(parts[g * HD:(g + 1) * HD, m, at:at + 2, :])).then_inc(st_q[L][min(m, 1)], 16)

                def rows(h, name, n=1):
                    return D[bass.ds(h, 1)].rearrange("h s d n -> (h s d) n")[slot[name] * HD:(slot[name] + n) * HD, :]

                def load_m(h, b):
                    wait(sp, sm_ok[L], 2 * TT * (h - 1))
                    sp.sem_inc(m_free, 1)
                    kr = 3 if L == 0 else 1
                    sp.dma_start(f(qm[b][0:kr * HD, :]), rows(h, "Q_HI", kr)).then_inc(ld_m[L][b], 16)
                    sp.dma_start(f(km[b][0:HD, :]), rows(h, "K_HI")).then_inc(ld_m[L][b], 16)

                def load_a(h, b):
                    wait(sp, st_ok[L], TT * (h - 1))
                    sp.sem_inc(a_free, 1)
                    sp.dma_start(f(qa[b][0:2 * HD, :]), rows(h, "Q_LO", 2)).then_inc(ld_a[L][b], 16)
                    sp.dma_start(f(qa[b][2 * HD:3 * HD, :]), rows(h, "Q_HI")).then_inc(ld_a[L][b], 16)
                    sp.dma_start(f(ka[b][0:HD, :]), rows(h, "K_HI")).then_inc(ld_a[L][b], 16)
                    sp.dma_start(f(ka[b][HD:3 * HD, :]), rows(h, "K_HI", 2)).then_inc(ld_a[L][b], 16)
                    if L == 0:
                        sp.dma_start(f(qb[b][:]), rows(h, "RH_HI", 4)).then_inc(ld_a[L][b], 16)

                def store(h, b, k, q=None):
                    tile = k // 4 if q is None else sp.snap(q + k // 4)
                    sp.wait_ge(o_ok[L], h + 1)
                    for r in range(4):
                        store_quarter(sp, L, b, k % 4, tile, r)

                def first_heads():
                    load_m(0, 0)
                    load_a(0, 0)
                    load_m(1, 1)
                    load_a(1, 1)

                if L == 1:
                    sp.wait_ge(pv_ok[0], TT * NH)
                for m in range(KT):
                    store_qk(m)
                    if m == 0 and L == 1:
                        sp.wait_ge(st_q[1][0], 16 * 8)
                        first_heads()
                if L == 0:
                    def store_rel(h, w=None):
                        names, part = (slice(0, 4), slice(0, 4)) if w is None else (slice(w, 4, 2), slice(w, 4, 2))
                        sp.dma_start(D[h, slot["RH_HI"]:slot["RH_HI"] + 4][names].rearrange("s d n -> d s n"),
                                     f(parts[h % 4:P:4, h // 4, part])).then_inc(st_r[min(h // 2, 1)], 16)

                    sp.wait_ge(rel_ev, 8)
                    for h in range(4):
                        store_rel(h, 0)
                    sp.wait_ge(rel_ev, 16)
                    for h in range(2):
                        store_rel(h, 1)
                    sp.wait_ge(st_q[0][0], 16 * 8)
                    sp.wait_ge(st_r[0], 16 * 4)
                    first_heads()
                    for h in range(2, 4):
                        store_rel(h, 1)
                    for h in range(4, NH):
                        store_rel(h)
                    sp.wait_ge(st_r[1], 16 * NH)
                sp.wait_ge(st_q[L][1], 16 * 16)
                load_m(2, 0)
                load_a(2, 0)
                load_m(3, 1)
                store(0, 0, 0)
                with sp.Fori(0, (NH - 4) // 4) as q:
                    for n in range(4):
                        h = q * 4 + n + 3
                        load_m(h + 1, n % 2)
                        load_a(h, 1 - n % 2)
                        if L == 1:
                            for out, at, size in ((xs_dram, 0, ZERO), (ys_dram, 2 * TT, ZERO // 2)):
                                tiles = out.rearrange("(t p) c -> p t c", p=P)
                                sp.dma_start(tiles[:, bass.ds(q * (4 * size) + at + n * size, size), :],
                                             zero[:].unsqueeze(1).broadcast_to([P, size, C])).then_inc(zero_st, 16)
                        store(h - 2, 1 - n % 2, n + 1, q)
                load_a(NH - 1, 1)
                if L == 1:
                    sp.wait_ge(pj_mm[0], TT)
                sp.dma_start(wproj[:], a[f"wproj{L}"].rearrange("(k p) n -> p k n", p=P)).then_inc(ld_p[L], 16)
                if L == 0:
                    load_wqkv(1)
                else:
                    load_expert(sp, 0, 0)
                for h in range(NH - 3, NH - 1):
                    store(h, h % 2, h)
                sp.wait_ge(o_ok[L], NH)
                for r in range(2):
                    store_quarter(sp, L, 1, 3, KT - 1, r)

            sp.wait_ge(pj_mm[1], TT)
            for dst, name in ((first[:], "low"), (above[:], "above")):
                sp.dma_start(dst, a[name]).then_inc(ld_g, 16)
            load_expert(sp, 1, 1)
            load_biases(sp, 0, 0)
            load_biases(sp, 1, 1)
            sp.wait_ge(scattered, 16 * 2 * TT)
            sp.dma_start(xs[:], xs_dram[0:P, :]).then_inc(x_ld, 16)
            sp.wait_ge(x_mm, 1)
            sp.dma_start(xs[:], xs_dram[P:2 * P, :]).then_inc(x_ld, 16)
            sp.wait_ge(cum_ok, 1)
            for e in range(NE):
                begin = sp.value_load(cum_i[0:1, e:e + 1], min_val=e, max_val=TILES)
                end = sp.value_load(cum_i[0:1, e + 1:e + 2], min_val=e + 1, max_val=TILES)
                with sp.Fori(begin, end) as j:
                    ahead = sp.snap(j * P + 2 * P)
                    here = sp.snap(j * P)
                    sp.wait_ge(x_mm, j + 2)
                    sp.dma_start(xs[:], xs_dram[bass.ds(ahead, P), :]).then_inc(x_ld, 16)
                    sp.wait_ge(y_ev, j + 2)
                    sp.dma_start(ys_dram[bass.ds(here, P), :], ysb[:]).then_inc(y_st, 16)
            sp.wait_ge(y_st, end * 16 + 16)
            sp.sem_inc(y_all, 1)
            for tt in range(TT):
                sp.wait_ge(t_out, 2 * tt + 2)
                sp.dma_start(a["out"][tt * P:(tt + 1) * P, :], t[:, tt, :]).then_inc(out_st, 16)
            sp.wait_ge(out_st, 16 * TT)

        @block.gpsimd
        def _(pool):
            def split_expert(e):
                b = e % 2
                for q in range(WQ):
                    pool.wait_ge(ld_1[b][WQ + q], 16 * (e // 2 + 1))
                    pool.tensor_scalar(piece2(w2_hi[b], q), piece2(w2_raw[b], q), 1.0, 1.0, ALU.mult, ALU.mult).then_inc(w2_hi_ok[b], 1)
                    pool.wait_ge(w2_hi_ok[b], WQ * (e // 2) + q + 1)
                    pool.tensor_tensor(piece2(w2_lo[b], q), piece2(w2_raw[b], q), f(piece2(w2_hi[b], q)), ALU.subtract).then_inc(w2_ok[b], 1)

            for L in L2:
                def add_tiles(h, b, last=False):
                    for n in range(1, ADDS[L] + 1):
                        if n == 2 and not last:
                            take_v(h + 1, 1 - b)
                        pool.wait_ge(p_ok[L], TT * h + n + 1)
                        if n == 1:
                            wait(pool, s_ok[L], h - 1)
                        wait(pool, va_ok[L], h + 1 if n < 2 or last else h + 2)
                        pool.sem_inc(p_in, 1)
                        if n == 1:
                            pool.tensor_tensor(acc[b], prob[:, 0, :], prob[:, 1, :], ALU.add).then_inc(a_ok[L], 1)
                        else:
                            pool.wait_ge(a_ok[L], ADDS[L] * h + n - 1)
                            pool.sem_inc(p_in, 1)
                            pool.tensor_tensor(acc[b], acc[b], prob[:, n % NP, :], ALU.add).then_inc(a_ok[L], 1)

                def take_v(h, b):
                    cols = bass.ds(h * HD, HD)
                    if isinstance(h, int) and h == 0:
                        pool.wait_ge(v_ev[L], TT)
                    wait(pool, pv_ok[L], TT * (h - 1))
                    wait(pool, a_ok[L], ADDS[L] * (h - 1) + 1 if not isinstance(h, int) or h else 0)
                    pool.sem_inc(p_in, 1)
                    pool.tensor_copy(va[b][:], vf[:, :, cols]).then_inc(va_ok[L], 1)

                take_v(0, 0)
                add_tiles(0, 0)
                add_tiles(1, 1)
                with pool.Fori(0, (NH - 4) // 4) as q:
                    for n in range(4):
                        add_tiles(q * 4 + n + 2, n % 2)
                add_tiles(NH - 2, 0)
                add_tiles(NH - 1, 1, last=True)

            pool.wait_ge(pv_ok[1], TT * NH)
            for i in L2:
                pool.wait_ge(st_o[1][i], 64 * NH // 2)
            split_expert(0)
            pool.wait_ge(where_ok, 1)
            pool.wait_ge(zero_st, 16 * 2 * (NH - 4))
            for r in range(2):
                for tt in range(TT):
                    pool.indirect_dma_start(
                        out=xs_dram[:, :], out_offset=bass.IndirectOffsetOnAxis(ap=where_i[:, r, tt:tt + 1], axis=0),
                        in_=tn[:, tt, :], in_offset=None).then_inc(scattered, 16)
            for e in range(1, NE):
                split_expert(e)
            pool.wait_ge(y_all, 1)
            for tt in range(TT):
                for r in range(2):
                    pool.indirect_dma_start(
                        out=gy[:, r, tt, :], out_offset=None, in_=ys_dram[:, :],
                        in_offset=bass.IndirectOffsetOnAxis(ap=where_i[:, r, tt:tt + 1], axis=0)).then_inc(gathered[tt], 16)

        @block.tensor
        def _(pe):
            mm = pe.matmul
            for r in range(2):
                pe.wait_ge(gn_ok, r + 1)
                if r == 0:
                    pe.wait_ge(ld_grp, 16)
                for m in range(KT):
                    for k in range(KT):
                        last = mm(ps[:, r, m:m + 1], grp[:, k * KT + m, :], mv[:, k, 0:1] if r == 0 else gd[:, k:k + 1],
                                  start=(k == 0), stop=(k == KT - 1))
                last.then_inc(g_sum, 1)

            for L in L2:
                pe.wait_ge(ld_w[L], 16)
                for u in range(2 * KT):
                    col = u // 2 + KT * (u % 2)
                    wait(pe, qk_ev[L], u - 1)
                    for half in range(2):
                        if u == 0:
                            pe.wait_ge(xn_ok[L], KT if L == 0 else TT // 2 * (half + 1))
                        for k in range(KT):
                            last = mm(ps[:, 2 * (u % 2) + half, :], wqkv[:, k, col * P:(col + 1) * P],
                                      xnT[:, k, half * HALF:(half + 1) * HALF], start=(k == 0), stop=(k == KT - 1))
                    last.then_inc(qk_mm[L], 1)

                n_m, n_a = (2, 5) if L == 0 else (2, 4)
                kr = 96 if L == 0 else 32

                def max_scores(h, b, qt):
                    if qt == 0:
                        pe.wait_ge(ld_m[L][b], (h - b) * 8 * n_m + 16 * n_m)
                    for half in range(2):
                        wait(pe, mx_ok[L], 2 * (TT * h + qt) + half - 1)
                        mm(ps[:, half, :], qm[b][0:kr, qt * P:(qt + 1) * P],
                           km[b][0:kr, half * HALF:(half + 1) * HALF], start=True, stop=True).then_inc(sm_ok[L], 1)

                def turn_max(h, b):
                    pe.wait_ge(mc_ok[L], h + 1)
                    wait(pe, r_ok[L], h)
                    pe.transpose(ps[0:TT, 7, 0:P], mcol[:, b, :], ident[:]).then_inc(mT_ok[L], 1)

                def scores(h, b, s):
                    if s == 0:
                        pe.wait_ge(ld_a[L][b], (h - b) * 8 * n_a + 16 * n_a)
                        pe.wait_ge(r_ok[L], h + 1)
                    wait(pe, p_ok[L], TT * h + s - 1)
                    for half in range(2):
                        out = ps[:, 2 + 2 * (s % 2) + half, :]
                        cols = slice(half * HALF, (half + 1) * HALF)
                        last = mm(out, ka[b][:, s * P:(s + 1) * P], qa[b][:, cols], start=True, stop=(L == 1))
                        if L == 0:
                            last = mm(out, eb[:, s * P:(s + 1) * P], qb[b][:, cols], start=False, stop=True)
                    last.then_inc(st_ok[L], 1)

                def quarters(half, lhs, src, start, stop):
                    for r in range(4):
                        last = mm(ps[HD * r:HD * (r + 1), 6, half * QUARTER:(half + 1) * QUARTER], lhs,
                                  src[:, r * QUARTER:(r + 1) * QUARTER], start=start, stop=stop, skip_group_check=True)
                    return last

                def out_product(h, b, s):
                    pe.wait_ge(p_ok[L], TT * h + s + 1)
                    if s == 0:
                        wait(pe, vs_ok[L], h)
                        pe.wait_ge(va_ok[L], h + 1)
                    last = quarters(0, va[b][:, s, :], prob[:, s % NP, :], s == 0, s == TT - 1)
                    if s > ADDS[L]:
                        last = quarters(1, ones[:, 0:HD], prob[:, s % NP, :], False, False)
                    last.then_inc(pv_ok[L], 1)

                def sums(h, b):
                    pe.wait_ge(a_ok[L], ADDS[L] * (h + 1))
                    quarters(1, ones[:, 0:HD], acc[b], False, True).then_inc(s_ok[L], 1)

                def head(h, b, first=False, left=2):
                    for s in range(TT):
                        scores(h, b, s)
                        for later, qt in (MAXIMA_FIRST if first else MAXIMA)[s]:
                            if left >= later:
                                max_scores(h + later, b if later == 2 else 1 - b, qt)
                        if s >= BEHIND:
                            out_product(h, b, s - BEHIND)
                        elif not first:
                            out_product(h - 1, 1 - b, TT + s - BEHIND)
                        if s == BEHIND - 1 and not first:
                            sums(h - 1, 1 - b)
                        if s == TT - AHEAD and left >= 1:
                            turn_max(h + 1, 1 - b)

                def first_maxima(maxima):
                    for h, m in maxima:
                        if h == m == 0:
                            pe.wait_ge(qk_ev[L], 2 * KT)
                            if L == 0:
                                pe.wait_ge(rel_ev, 16)
                                pe.wait_ge(ld_e, 32)
                        max_scores(h, h, m)

                def values(tt):
                    if tt == 0:
                        pe.wait_ge(ld_v[L], 16)
                    wait(pe, v_ev[L], tt - 2)
                    for k in range(KT):
                        last = mm(ps[:, 4 + tt % 3, 0:C], xnT[:, k, tt * P:(tt + 1) * P],
                                  wqkv[:, k, 2 * C:3 * C], start=(k == 0), stop=(k == KT - 1))
                        if k == 0:
                            first_maxima(BETWEEN[L][tt][0:1] if len(BETWEEN[L][tt]) == 2 else [])
                    last.then_inc(v_mm[L], 1)
                    first_maxima(BETWEEN[L][tt][1:] if len(BETWEEN[L][tt]) == 2 else BETWEEN[L][tt])

                for tt in range(EARLY[L]):
                    values(tt)
                if L == 0:
                    pe.wait_ge(qk_ev[0], 2 * KT)
                    pe.wait_ge(bd_ok, 4)
                    for w in range(2):
                        for i in range(SIDE // 4):
                            n = 8 * w + i
                            wait(pe, rel_ev, n - 3)
                            for j in range(4):
                                s = 4 * i + j
                                q = qf[:, :, :].rearrange("p g (h w) -> p g h w", w=SIDE)
                                rhs = q[:, :, s, :] if w == 0 else q[:, :, :, s]
                                last = mm(ps[:, n % 4, 96 * j:96 * j + 96], bd[:, w, SIDE - 1 - s:REL - s, :].rearrange("p i a -> p (i a)"),
                                          rhs, start=True, stop=True)
                            last.then_inc(rel_mm, 1)

                for tt in range(EARLY[L], TT):
                    values(tt)
                    if tt == TURN[L]:
                        turn_max(0, 0)
                pe.wait_ge(v_ev[L], TT)
                head(0, 0, first=True)
                head(1, 1)
                with pe.Fori(0, (NH - 4) // 4) as q:
                    for n in range(4):
                        head(q * 4 + n + 2, n % 2)
                head(NH - 2, 0, left=1)
                head(NH - 1, 1, left=0)
                for s in range(TT - BEHIND, TT):
                    out_product(NH - 1, 1, s)
                sums(NH - 1, 1)

                def project(tt, ks):
                    for k in ks:
                        last = mm(ps[:, tt % 4, 0:C], oT[:, k, tt * P:(tt + 1) * P], wproj[:, k, :],
                                  start=(k == 0), stop=(k == KT - 1))
                    return last

                pe.wait_ge(ld_p[L], 16)
                pe.wait_ge(o_ok[L], NH - 2)
                pe.wait_ge(p_ok[L], TT * NH)
                for tt in range(4):
                    project(tt, (0, 1))
                for i in L2:
                    pe.wait_ge(st_o[L][i], 64 * NH // 2)
                def turn_stream(tt):
                    pe.wait_ge(tn_ok[L], tt + 1)
                    wait(pe, xn_ok[L + 1], tt - 1)
                    for k in range(KT):
                        last = pe.transpose(ps[:, 4 + tt % 2, k * P:(k + 1) * P], tn[:, tt, k * P:(k + 1) * P], ident[:])
                    last.then_inc(tr_mm[L], 1)

                def gate_tile(tt):
                    pe.wait_ge(xn_ok[2], tt + 1)
                    for k in range(KT):
                        last = mm(ps[:, 6, tt * NE:(tt + 1) * NE], xnT[:, k, tt * P:(tt + 1) * P], gate[:, k, :],
                                  start=(k == 0), stop=(k == KT - 1))
                    if tt == TT - 1:
                        last.then_inc(lg_mm, 1)

                for tt in range(TT + 3):
                    if tt < TT:
                        wait(pe, t_ok[L], tt - 3)
                        project(tt, range(KT) if tt >= 4 else (2,)).then_inc(pj_mm[L], 1)
                    if 2 <= tt < TT + 2:
                        turn_stream(tt - 2)
                    if tt >= 3 and L == 1:
                        gate_tile(tt - 3)

            pe.wait_ge(sel_ok, 1)
            mm(ps[:, 7, 0:(TT + 1) * NE], before[:], taken[:], start=True, stop=False)
            for tt in range(TT):
                rest = TT - tt
                last = mm(ps[:, 7, (tt + 1) * NE:(TT + 1) * NE], ones[:],
                          taken[:, tt:tt + 1, :].broadcast_to([P, rest, NE]), start=False, stop=(tt == TT - 1))
            last.then_inc(cnt_mm, 1)

            def turn(n):
                pe.wait_ge(x_ld, 16 * n + 16)
                wait(pe, x_ok, n)
                for k in range(KT):
                    last = pe.transpose(ps[:, 7, k * P:(k + 1) * P], xs[:, k * P:(k + 1) * P], ident[:])
                last.then_inc(x_mm, 1)

            pe.wait_ge(cum_ok, 1)
            pe.wait_ge(where_ok, 1)
            turn(0)
            with pe.Fori(0, NE // 2) as pair:
                for b in L2:
                    e = pair * 2 + b
                    begin = pe.value_load(cum_i[0:1, bass.ds(e, 1)], min_val=0, max_val=TILES - 1)
                    end = pe.value_load(cum_i[0:1, bass.ds(e + 1, 1)], min_val=1, max_val=TILES)
                    with pe.Fori(begin, end) as j:
                        pe.wait_ge(x_ok, j + 1)
                        for g in range(HGS):
                            pe.wait_ge(ld_1[b][g * WQ // HGS], pair * 16 + 16)
                            pe.wait_ge(h_f_ok, j * HGS + g + 1)
                            for c in range(g * HG, (g + 1) * HG):
                                for k in range(KT):
                                    last = mm(ps[:, g, c % HG * P:(c % HG + 1) * P], w1[b][:, k, c * P:(c + 1) * P],
                                              xT[:, k, :], start=(k == 0), stop=(k == KT - 1))
                            last.then_inc(h_mm, 1)
                        turn(j + 1)
                        pe.wait_ge(y_ev, j + 1)
                        for c in range(HC):
                            if c % WC == 0:
                                pe.wait_ge(w2_ok[b], pair * WQ + c // WC + 1)
                            if c % HG == 0:
                                pe.wait_ge(h_l_ok, j * HGS + c // HG + 1 + HGS)
                            for n, (h, w) in enumerate(((h_hi, w2_hi[b]), (h_hi, w2_lo[b]), (h_lo, w2_hi[b]))):
                                last = mm(ps[:, 6, 0:C], h[:, c, :], w[:, c, :],
                                          start=(c == 0 and n == 0), stop=(c == HC - 1 and n == 2))
                        last.then_inc(y_mm, 1)

        @block.vector
        def _(v):
            done = [0]

            def own(ins):
                done[0] += 1
                ins.then_inc(dv, 1)
                v.wait_ge(dv, done[0])

            own(v.memset(bd[:], 0.0))
            for i in L2:
                v.memset(f(ka[i][96:104, :]), 1.0)
            v.memset(zero[:], 0.0)
            v.memset(eps[:], 1e-5)
            v.memset(spare[:], 1.0)
            v.memset(ones[:], 1.0).then_inc(made, 1)
            v.sem_inc(y_ev, 1)
            v.sem_inc(y_st, 16)
            v.sem_inc(h_f_ok, HGS)
            v.sem_inc(h_l_ok, HGS)
            for k in range(KT):
                v.wait_ge(ld_x[k], 16)
                for half in range(2):
                    own(v.bn_stats(stat[:, k, 6 * half:6 * half + 6], xnT[:, k, half * HALF:(half + 1) * HALF]))
                own(v.bn_aggr(mv[:, k, :], stat[:, k, :]))
            v.sem_inc(gn_ok, 1)
            v.wait_ge(g_sum, 1)
            own(v.tensor_copy(gm[:, :, 0], ps[:, 0, 0:KT]))
            own(v.tensor_tensor(gd[:], mv[:, 0:KT, 0], gm[:, :, 0], ALU.subtract))
            own(v.tensor_tensor(gd[:], gd[:], gd[:], ALU.mult))
            own(v.tensor_tensor(gd[:], gd[:], mv[:, 0:KT, 1], ALU.add))
            v.sem_inc(gn_ok, 1)
            v.wait_ge(g_sum, 2)
            v.tensor_scalar(gm[:, :, 1], ps[:, 1, 0:KT], 1e-5, None, ALU.add).then_inc(lx, 1)
            v.wait_ge(av, 1)
            own(v.reciprocal(rstd[:, 0:KT], sd[:, 0:KT]))
            for k in range(KT):
                v.tensor_scalar(xnT[:, k, :], xnT[:, k, :], gm[:, k, 0:1], rstd[:, k:k + 1],
                                ALU.subtract, ALU.mult).then_inc(xn_ok[0], 1)

            v.wait_ge(ld_c, 16 * 17)
            v.tensor_copy(eb[:], ebf).then_inc(eb_ok, 1)
            for g in range(4):
                part = slice(g * HD, (g + 1) * HD)
                v.tensor_copy(bd[part, :, :, g], tab[part]).then_inc(bd_ok, 1)

            for L in L2:
                if L == 1:
                    v.wait_ge(st_r[0], 16 * 4)
                    v.wait_ge(st_r[1], 16 * NH)
                for u in range(2 * KT):
                    m = u // 2
                    src, s = (qf[:, m, :], SCALE[L]) if u % 2 == 0 else (kf[:, m % 2, :], 1.0)
                    lo, hi = (parts[:, m, 0, :], parts[:, m, 1, :]) if u % 2 == 0 else (parts[:, m, 3, :], parts[:, m, 2, :])
                    v.wait_ge(qk_ev[L], u + 1)
                    v.tensor_scalar(hi, src, s, None, ALU.mult).then_inc(split[L], 1)
                    v.wait_ge(split[L], 2 * u + 1)
                    v.scalar_tensor_tensor(lo, src, s, f(hi), ALU.mult, ALU.subtract).then_inc(split[L], 1)

                def values(tt):
                    v.wait_ge(v_mm[0], tt + 1)
                    v.tensor_tensor(vf[:, tt, :], ps[:, 4 + tt % 3, 0:C], bv[:], ALU.add).then_inc(v_ev[0], 1)

                for tt in range(EARLY[L]):
                    values(tt)
                if L == 0:
                    for w in range(2):
                        hi, lo = (parts[:, :, i, :].rearrange("p m (h w) -> p m h w", w=SIDE) for i in (w, 2 + w))
                        for i in range(SIDE // 4):
                            v.wait_ge(rel_hi, 8 * w + i + 1)
                            v.tensor_tensor(rel_tile(lo, w, i), rel_bank(w, i), f(rel_tile(hi, w, i)), ALU.subtract).then_inc(rel_ev, 1)
                def maximum(h, b, qt):
                    for half in range(2):
                        v.wait_ge(sm_ok[L], 2 * (TT * h + qt) + half + 1)
                        v.tensor_reduce(mhalf[:, b, qt, half:half + 1], ps[:, half, :], AX.X, ALU.max).then_inc(mx_ok[L], 1)
                    if qt == TT - 1:
                        v.wait_ge(mx_ok[L], 2 * TT * (h + 1))
                        wait(v, mT_ok[L], h - 1)
                        v.tensor_reduce(mcol[:, b, :], mhalf[:, b], AX.X, ALU.max).then_inc(mc_ok[L], 1)

                def invert_sums(h, part):
                    v.wait_ge(vs_ok[L], h + 1)
                    wait(v, o_ok[L], h)
                    cols = slice(part * QUARTER // 4, (part + 1) * QUARTER // 4)
                    v.reciprocal(rec[:, cols], vsb[:, 1, cols]).then_inc(o_rc[L], 1)

                def output(h, b):
                    wait(v, st_o[L][b], 32 * (h - b))
                    v.wait_ge(o_rc[L], 4 * (h + 1))
                    v.tensor_tensor(osb[b][:], vsb[:, 0, :], rec[:], ALU.mult).then_inc(o_ok[L], 1)

                def head(h, b, first=False, left=2):
                    for s in range(TT):
                        for later, qt in (MAXIMA_FIRST if first else MAXIMA)[s]:
                            if left >= later:
                                maximum(h + later, b if later == 2 else 1 - b, qt)
                        if 3 <= s < 7 and not first:
                            invert_sums(h - 1, s - 3)
                        if s == 6 and not first:
                            output(h - 1, 1 - b)

                for tt in range(EARLY[L], TT):
                    if L == 0:
                        values(tt)
                    for h, m in BETWEEN[L][tt]:
                        maximum(h, h, m)
                head(0, 0, first=True)
                head(1, 1)
                with v.Fori(0, (NH - 4) // 4) as q:
                    for n in range(4):
                        head(q * 4 + n + 2, n % 2)
                head(NH - 2, 0, left=1)
                if L == 0:
                    v.wait_ge(ld_t, 16)
                v.tensor_tensor(t[:], t[:], bproj[:, L:L + 1, :].broadcast_to([P, TT, C]), ALU.add).then_inc(tb_ok, 1)
                head(NH - 1, 1, left=0)
                for part in range(4):
                    invert_sums(NH - 1, part)
                output(NH - 1, 1)

                v.wait_ge(tb_ok, L + 1)
                for tt in range(TT + 1):
                    if tt < TT:
                        v.wait_ge(pj_mm[L], tt + 1)
                        v.tensor_tensor(t[:, tt, :], t[:, tt, :], ps[:, tt % 4, 0:C], ALU.add).then_inc(t_ok[L], 1)
                        v.wait_ge(t_ok[L], tt + 1)
                        own(v.bn_stats(stat[:, tt, 0:6], t[:, tt, :]))
                        v.bn_aggr(mv[:, tt, :], stat[:, tt, 0:6]).then_inc(var_ok[L], 1)
                    if tt > 0:
                        v.wait_ge(sq_ok[L], tt)
                        own(v.reciprocal(rstd[:, tt - 1:tt], sd[:, tt - 1:tt]))
                        v.tensor_scalar(tn[:, tt - 1, :], t[:, tt - 1, :], mv[:, tt - 1, 0:1], rstd[:, tt - 1:tt],
                                        ALU.subtract, ALU.mult).then_inc(tn_ok[L], 1)

            v.wait_ge(lg_mm, 1)
            own(v.tensor_tensor(lg[:], ps[:, 6, 0:TT * NE].rearrange("p (t e) -> p t e", e=NE),
                                gateb[:].unsqueeze(1).broadcast_to([P, TT, NE]), ALU.add))
            own(v.tensor_reduce(m8[:], lg[:], AX.X, ALU.max))
            v.tensor_tensor(lg[:], lg[:], m8[:].unsqueeze(2).broadcast_to([P, TT, NE]), ALU.subtract).then_inc(lx, 1)
            v.wait_ge(av, 2)
            own(v.tensor_reduce(s8[:], pr[:], AX.X, ALU.add))
            own(v.reciprocal(s8[:], s8[:]))
            own(v.tensor_tensor(pr[:], pr[:], s8[:].unsqueeze(2).broadcast_to([P, TT, NE]), ALU.mult))
            mine = pr[:].unsqueeze(3).broadcast_to([P, TT, NE, NE])
            other = pr[:].unsqueeze(2).broadcast_to([P, TT, NE, NE])
            own(v.tensor_tensor(cm[:], other, mine, ALU.is_gt))
            own(v.tensor_tensor(cm2[:], other, mine, ALU.is_equal))
            v.wait_ge(ld_g, 32)
            own(v.tensor_tensor(cm2[:], cm2[:], first[:].unsqueeze(1).broadcast_to([P, TT, NE, NE]), ALU.mult))
            own(v.tensor_tensor(cm[:], cm[:], cm2[:], ALU.add))
            own(v.tensor_reduce(rk[:], cm[:], AX.X, ALU.add))
            own(v.memset(taken[:], 0.0))
            own(v.tensor_scalar(taken[:, 0:TT, :], rk[:], 1.5, None, ALU.is_lt))
            v.sem_inc(sel_ok, 1)
            own(v.tensor_scalar(choice[:, 0], rk[:], 0.5, None, ALU.is_lt))
            own(v.tensor_tensor(choice[:, 1], taken[:, 0:TT, :], choice[:, 0], ALU.subtract))
            own(v.tensor_tensor(w8[:], taken[:, 0:TT, :], pr[:], ALU.mult))
            own(v.tensor_reduce(s8[:], w8[:], AX.X, ALU.add))
            own(v.reciprocal(s8[:], s8[:]))
            own(v.tensor_tensor(w8[:], w8[:], s8[:].unsqueeze(2).broadcast_to([P, TT, NE]), ALU.mult))
            own(v.tensor_tensor(prod[:], choice[:], w8[:].unsqueeze(1).broadcast_to([P, 2, TT, NE]), ALU.mult))
            own(v.tensor_reduce(wts[:], prod[:], AX.X, ALU.add))
            v.wait_ge(cnt_mm, 1)
            places = ps[:, 7, 0:TT * NE].rearrange("p (t e) -> p t e", e=NE)
            count = ps[:, 7, TT * NE:(TT + 1) * NE]
            own(v.tensor_tensor(cm[:, 0], count.unsqueeze(2).broadcast_to([P, NE, NE]), above[:], ALU.is_gt))
            own(v.tensor_reduce(ntile[:], cm[:, 0], AX.X, ALU.add))
            own(v.tensor_tensor(cm[:, 1], first[:], ntile[:].unsqueeze(1).broadcast_to([P, NE, NE]), ALU.mult))
            own(v.tensor_reduce(cum[:, 0:NE], cm[:, 1], AX.X, ALU.add))
            own(v.tensor_tensor(cum[:, NE:NE + 1], cum[:, NE - 1:NE], ntile[:, NE - 1:NE], ALU.add))
            own(v.tensor_copy(cum_i[:], cum[:]))
            v.sem_inc(cum_ok, 1)
            own(v.tensor_scalar(cum[:], cum[:], float(P), None, ALU.mult))
            own(v.tensor_tensor(slot[:], places, cum[:, 0:NE].unsqueeze(1).broadcast_to([P, TT, NE]), ALU.add))
            own(v.tensor_tensor(prod[:], choice[:], slot[:].unsqueeze(1).broadcast_to([P, 2, TT, NE]), ALU.mult))
            own(v.tensor_reduce(where[:], prod[:], AX.X, ALU.add))
            own(v.tensor_copy(where_i[:], where[:]))
            v.sem_inc(where_ok, 1)

            with v.Fori(0, NE // 2) as pair:
                for b in L2:
                    e = pair * 2 + b
                    begin = v.value_load(cum_i[0:1, bass.ds(e, 1)], min_val=0, max_val=TILES - 1)
                    end = v.value_load(cum_i[0:1, bass.ds(e + 1, 1)], min_val=1, max_val=TILES)
                    with v.Fori(begin, end) as j:
                        for g in range(HGS):
                            cs = slice(g * HG, (g + 1) * HG)
                            v.wait_ge(h_f_ok, j * HGS + g + 1 + HGS)
                            v.tensor_copy(h_hi[:, cs, :], h_f[:, cs, :]).then_inc(h_h_ok, 1)
                            v.wait_ge(h_h_ok, j * HGS + g + 1)
                            v.tensor_tensor(h_lo[:, cs, :], h_f[:, cs, :], f(h_hi[:, cs, :]), ALU.subtract).then_inc(h_l_ok, 1)
                        v.wait_ge(y_mm, j + 1)
                        v.wait_ge(ld_b[b], pair * 32 + 32)
                        v.wait_ge(y_st, j * 16 + 16)
                        v.tensor_tensor(ysb[:], ps[:, 6, 0:C], b2c[b][:], ALU.add).then_inc(y_ev, 1)

            for tt in range(TT):
                v.wait_ge(gathered[tt], 32)
                for r in range(2):
                    v.scalar_tensor_tensor(t[:, tt, :], gy[:, r, tt, :], wts[:, r, tt:tt + 1], t[:, tt, :],
                                           ALU.mult, ALU.add).then_inc(t_out, 1)
                    v.wait_ge(t_out, 2 * tt + r + 1)

        @block.scalar
        def _(act):
            act.wait_ge(lx, 1)
            act.activation(sd[:, 0:KT], gm[:, :, 1], ACT.Sqrt).then_inc(av, 1)
            act.wait_ge(ld_bq, 16)
            for L in L2:
                for u in range(2 * KT):
                    m = u // 2
                    act.wait_ge(qk_mm[L], u + 1)
                    if u == 5:
                        act.wait_ge(split[L], 4)
                    dst = qf[:, m, :] if u % 2 == 0 else kf[:, m % 2, :]
                    src = ps[:, 2 * (u % 2):2 * (u % 2) + 2, :].rearrange("p a b -> p (a b)")
                    if L == 0:
                        col = m + KT * (u % 2)
                        act.activation(dst, src, ACT.Identity, bias=bqk[:, col:col + 1]).then_inc(qk_ev[L], 1)
                    else:
                        act.activation(dst, src, ACT.Copy).then_inc(qk_ev[L], 1)
                if L == 0:
                    act.wait_ge(st_q[0][0], 16 * 8)
                    act.wait_ge(st_q[0][1], 16 * 16)
                    for w in range(2):
                        hi = parts[:, :, w, :].rearrange("p m (h w) -> p m h w", w=SIDE)
                        for i in range(SIDE // 4):
                            act.wait_ge(rel_mm, 8 * w + i + 1)
                            act.activation(rel_tile(hi, w, i), rel_bank(w, i), ACT.Copy).then_inc(rel_hi, 1)
                act.wait_ge(made, 1)
                act.activation(spare[:], spare[:], ACT.Exp)

                def head(h, b, first=False, last=False):
                    for s in range(TT):
                        act.wait_ge(st_ok[L], TT * h + s + 1)
                        if s >= NP or not first:
                            last_h, last_s = (h, s - NP) if s >= NP else (h - 1, max(n for n in range(TT) if n % NP == s))
                            act.wait_ge(pv_ok[L], TT * last_h + last_s + 1)
                            if last_s <= ADDS[L]:
                                act.wait_ge(a_ok[L], ADDS[L] * last_h + max(last_s, 1))
                        act.activation(prob[:, s % NP, :], ps[:, 2 + 2 * (s % 2):4 + 2 * (s % 2), :].rearrange("p a b -> p (a b)"),
                                       ACT.Exp).then_inc(p_ok[L], 1)
                        if TT - AHEAD <= s < TT - 1 and not last:
                            i = s - TT + AHEAD
                            place_max(h + 1, 1 - b, range(PLACED[i], PLACED[i + 1]))
                        if s == BEHIND - 1 and not first:
                            keep_output(h - 1)

                def place_max(h, b, tiles):
                    act.wait_ge(mT_ok[L], h + 1)
                    wait(act, st_ok[L], TT * (h - 1))
                    for i in tiles:
                        last = act.activation(qa[b][96:104, i * P:(i + 1) * P], ps[0:TT, 7, 0:P], ACT.Copy, scale=negd[:, i:i + 1])
                    if i == TT - 1:
                        last.then_inc(r_ok[L], 1)

                def keep_output(h):
                    act.wait_ge(s_ok[L], h + 1)
                    wait(act, o_ok[L], h)
                    act.activation(vsb[:].rearrange("p a b -> p (a b)"), ps[:, 6, :], ACT.Copy).then_inc(vs_ok[L], 1)

                for tt in range(TT):
                    if L == 1:
                        act.wait_ge(v_mm[1], tt + 1)
                        act.activation(vf[:, tt, :], ps[:, 4 + tt % 3, 0:C], ACT.Copy).then_inc(v_ev[1], 1)
                    if tt == TURN[L]:
                        place_max(0, 0, range(TT))
                head(0, 0, first=True)
                head(1, 1)
                with act.Fori(0, (NH - 4) // 4) as q:
                    for n in range(4):
                        head(q * 4 + n + 2, n % 2)
                head(NH - 2, 0)
                head(NH - 1, 1, last=True)
                keep_output(NH - 1)
                act.activation(spare[:], spare[:], ACT.Sqrt)
                act.wait_ge(o_ok[L], NH)
                for r in range(2, 4):
                    store_quarter(act, L, 1, 3, KT - 1, r)
                for tt in range(TT + 2):
                    if tt < TT:
                        act.wait_ge(var_ok[L], tt + 1)
                        act.activation(sd[:, tt:tt + 1], mv[:, tt, 1:2], ACT.Sqrt, bias=eps[:, 0:1]).then_inc(sq_ok[L], 1)
                    if tt >= 2:
                        act.wait_ge(tr_mm[L], tt - 1)
                        act.activation(xnT[:, :, (tt - 2) * P:(tt - 1) * P],
                                       ps[:, 4 + tt % 2, 0:C].rearrange("p (k q) -> p k q", k=KT), ACT.Copy).then_inc(xn_ok[L + 1], 1)
            act.activation(spare[:], spare[:], ACT.Exp)
            act.wait_ge(lx, 2)
            act.activation(pr[:], lg[:], ACT.Exp).then_inc(av, 1)

            def turned(n):
                act.wait_ge(x_mm, n + 1)
                act.activation(xT[:], ps[:, 7, 0:C].rearrange("p (k q) -> p k q", k=KT), ACT.Copy).then_inc(x_ok, 1)

            turned(0)
            act.wait_ge(cum_ok, 1)
            for e in range(NE):
                b = e % 2
                begin = act.value_load(cum_i[0:1, e:e + 1], min_val=e, max_val=TILES - 1)
                end = act.value_load(cum_i[0:1, e + 1:e + 2], min_val=e + 1, max_val=TILES)
                if 1 <= e < NE - 1:
                    act.wait_ge(y_ev, begin + 1)
                    load_expert(act, e + 1, 1 - b)
                    load_biases(act, e + 1, 1 - b)
                act.wait_ge(ld_b[b], 32 * (e // 2 + 1))
                with act.Fori(begin, end) as j:
                    for g in range(HGS):
                        act.wait_ge(h_mm, j * HGS + g + 1)
                        act.wait_ge(h_l_ok, j * HGS + g + 1)
                        for c in range(g * HG, (g + 1) * HG):
                            last = act.activation(h_f[:, c, :], ps[:, g, c % HG * P:(c % HG + 1) * P],
                                                  ACT.Relu, bias=b1c[b][:, c:c + 1])
                        last.then_inc(h_f_ok, 1)
                    turned(j + 1)


def constants():
    key = np.arange(N)
    rows = np.arange(SIDE)[:, None]
    pos = np.concatenate([key // SIDE == rows, key % SIDE == rows])
    group = np.arange(C) // GROUP
    same = (group[:, None] == group[None, :]) / np.float32(GROUP)
    blocks = same.reshape(KT, P, KT, P).transpose(0, 2, 1, 3).reshape(KT * KT, P, P)
    negd = -np.eye(TT, dtype=np.float32)
    low = np.broadcast_to(np.tril(np.ones((NE, NE)), -1), (P, NE, NE))
    above = np.broadcast_to(np.array([-1] + [i * P for i in range(1, NE)]), (P, NE, NE))
    return {
        "ident": np.eye(P, dtype=np.float32), "grp": blocks.astype(np.float32),
        "eb": np.concatenate([pos, pos]).astype(np.float32), "negd": negd,
        "low": np.ascontiguousarray(low, np.float32), "above": np.ascontiguousarray(above, np.float32),
        "before": np.triu(np.ones((P, P), np.float32), 1),
    }


def kernel(x, L0_conv_qkv_w, L0_conv_qkv_b, L0_conv_proj_w, L0_conv_proj_b, L0_conv_rel_pos_h, L0_conv_rel_pos_w,
           L1_attn_w_qkv, L1_attn_w_proj, L1_attn_b_proj, L1_ffn_gate_w, L1_ffn_gate_b, L1_ffn_w1, L1_ffn_b1,
           L1_ffn_w2, L1_ffn_b2):
    import concourse.bacc as bacc
    from concourse.bass_utils import run_bass_kernel_spmd as run

    tokens = np.asarray(x).reshape(N, C)
    arrays = {
        "x": tokens, "xT": tokens.T,
        "wqkv0": np.asarray(L0_conv_qkv_w).T, "wqkv1": np.asarray(L1_attn_w_qkv).T,
        "bqk": np.asarray(L0_conv_qkv_b)[:2 * C].reshape(2 * KT, P).T, "bv": np.asarray(L0_conv_qkv_b)[2 * C:],
        "wproj0": np.asarray(L0_conv_proj_w).T, "bproj0": np.asarray(L0_conv_proj_b),
        "wproj1": np.asarray(L1_attn_w_proj).T, "bproj1": np.asarray(L1_attn_b_proj),
        "relh": np.asarray(L0_conv_rel_pos_h)[::-1].T, "relw": np.asarray(L0_conv_rel_pos_w)[::-1].T,
        "gate": np.asarray(L1_ffn_gate_w).T, "gateb": np.asarray(L1_ffn_gate_b),
        "w1": np.asarray(L1_ffn_w1).transpose(0, 2, 1), "b1": np.asarray(L1_ffn_b1).reshape(NE, HC, P).transpose(0, 2, 1),
        "w2": np.asarray(L1_ffn_w2).transpose(0, 2, 1), "b2": np.asarray(L1_ffn_b2),
    }
    arrays.update(constants())
    arrays = {k: np.ascontiguousarray(v) for k, v in arrays.items()}
    nc = bacc.Bacc("TRN2", target_bir_lowering=False, num_devices=1)
    aps = {k: nc.dram_tensor(f"in_{k}", v.shape, mybir.dt.from_np(v.dtype), kind="ExternalInput").ap()
           for k, v in arrays.items()}
    aps["out"] = nc.dram_tensor("out_0", (N, C), F32, kind="ExternalOutput").ap()
    build_program(nc, aps)
    result = run(nc, [{f"in_{k}": v for k, v in arrays.items()}], core_ids=[0])
    return np.asarray(result.results[0]["out_0"]).reshape(np.shape(x))
```
